# Optimizing a Trainium2 kernel written in Bass

```python
import numpy as np
import jax
import jax.numpy as jnp

def _softmax(x, axis=-1):
    return jax.nn.softmax(x, axis=axis)

def _gelu(x):
    return jax.nn.gelu(x, approximate=True)

def _silu(x):
    return jax.nn.silu(x)

def _sigmoid(x):
    return jax.nn.sigmoid(x)

def _layernorm(x, axis=-1, eps=1e-05):
    m = jnp.mean(x, axis=axis, keepdims=True)
    v = jnp.var(x, axis=axis, keepdims=True)
    return (x - m) / jnp.sqrt(v + eps)

def _scatter_add(tgt, idx, src, axis=0):
    return tgt.at[idx].add(src)

def _segment_sum(src, seg, n):
    return jax.ops.segment_sum(src, seg, n)
kernel_name = 'mk_dlrm_tower_d1_rec_r8_5c25bf'

def setup_inputs(seed: int=0):
    np.random.seed(seed)
    _w = jnp.asarray

    def _rec_inputs():
        import jax
        import jax.numpy as jnp
        _tk = jax.random.key(seed)
        dense_ctx = jax.random.normal(jax.random.fold_in(_tk, 190), (1024, 16), jnp.float32)
        ids = jnp.stack([jax.random.randint(jax.random.fold_in(_tk, 200 + f), (1024,), 0, v, jnp.int32) for f, v in enumerate([12500, 1250, 1000, 12500, 12500, 12500, 125000, 125000, 125000, 125000, 1250, 125000, 1000, 1000, 125000, 1000, 1250, 125000, 12500, 12500, 1000, 1000, 125000, 1250, 1000, 1250, 1250, 125000, 12500, 1250, 125000, 1000, 12500, 1000, 1000, 12500, 125000, 1250, 1250])], axis=1)
        tbl_0 = 0.05 * jax.random.normal(jax.random.fold_in(_tk, 500 + 0), (12500, 16), jnp.float32)
        tbl_1 = 0.05 * jax.random.normal(jax.random.fold_in(_tk, 500 + 1), (1250, 16), jnp.float32)
        tbl_2 = 0.05 * jax.random.normal(jax.random.fold_in(_tk, 500 + 2), (1000, 16), jnp.float32)
        tbl_3 = 0.05 * jax.random.normal(jax.random.fold_in(_tk, 500 + 3), (12500, 16), jnp.float32)
        tbl_4 = 0.05 * jax.random.normal(jax.random.fold_in(_tk, 500 + 4), (12500, 16), jnp.float32)
        tbl_5 = 0.05 * jax.random.normal(jax.random.fold_in(_tk, 500 + 5), (12500, 16), jnp.float32)
        tbl_6 = 0.05 * jax.random.normal(jax.random.fold_in(_tk, 500 + 6), (125000, 16), jnp.float32)
        tbl_7 = 0.05 * jax.random.normal(jax.random.fold_in(_tk, 500 + 7), (125000, 16), jnp.float32)
        tbl_8 = 0.05 * jax.random.normal(jax.random.fold_in(_tk, 500 + 8), (125000, 16), jnp.float32)
        tbl_9 = 0.05 * jax.random.normal(jax.random.fold_in(_tk, 500 + 9), (125000, 16), jnp.float32)
        tbl_10 = 0.05 * jax.random.normal(jax.random.fold_in(_tk, 500 + 10), (1250, 16), jnp.float32)
        tbl_11 = 0.05 * jax.random.normal(jax.random.fold_in(_tk, 500 + 11), (125000, 16), jnp.float32)
        tbl_12 = 0.05 * jax.random.normal(jax.random.fold_in(_tk, 500 + 12), (1000, 16), jnp.float32)
        tbl_13 = 0.05 * jax.random.normal(jax.random.fold_in(_tk, 500 + 13), (1000, 16), jnp.float32)
        tbl_14 = 0.05 * jax.random.normal(jax.random.fold_in(_tk, 500 + 14), (125000, 16), jnp.float32)
        tbl_15 = 0.05 * jax.random.normal(jax.random.fold_in(_tk, 500 + 15), (1000, 16), jnp.float32)
        tbl_16 = 0.05 * jax.random.normal(jax.random.fold_in(_tk, 500 + 16), (1250, 16), jnp.float32)
        tbl_17 = 0.05 * jax.random.normal(jax.random.fold_in(_tk, 500 + 17), (125000, 16), jnp.float32)
        tbl_18 = 0.05 * jax.random.normal(jax.random.fold_in(_tk, 500 + 18), (12500, 16), jnp.float32)
        tbl_19 = 0.05 * jax.random.normal(jax.random.fold_in(_tk, 500 + 19), (12500, 16), jnp.float32)
        tbl_20 = 0.05 * jax.random.normal(jax.random.fold_in(_tk, 500 + 20), (1000, 16), jnp.float32)
        tbl_21 = 0.05 * jax.random.normal(jax.random.fold_in(_tk, 500 + 21), (1000, 16), jnp.float32)
        tbl_22 = 0.05 * jax.random.normal(jax.random.fold_in(_tk, 500 + 22), (125000, 16), jnp.float32)
        tbl_23 = 0.05 * jax.random.normal(jax.random.fold_in(_tk, 500 + 23), (1250, 16), jnp.float32)
        tbl_24 = 0.05 * jax.random.normal(jax.random.fold_in(_tk, 500 + 24), (1000, 16), jnp.float32)
        tbl_25 = 0.05 * jax.random.normal(jax.random.fold_in(_tk, 500 + 25), (1250, 16), jnp.float32)
        tbl_26 = 0.05 * jax.random.normal(jax.random.fold_in(_tk, 500 + 26), (1250, 16), jnp.float32)
        tbl_27 = 0.05 * jax.random.normal(jax.random.fold_in(_tk, 500 + 27), (125000, 16), jnp.float32)
        tbl_28 = 0.05 * jax.random.normal(jax.random.fold_in(_tk, 500 + 28), (12500, 16), jnp.float32)
        tbl_29 = 0.05 * jax.random.normal(jax.random.fold_in(_tk, 500 + 29), (1250, 16), jnp.float32)
        tbl_30 = 0.05 * jax.random.normal(jax.random.fold_in(_tk, 500 + 30), (125000, 16), jnp.float32)
        tbl_31 = 0.05 * jax.random.normal(jax.random.fold_in(_tk, 500 + 31), (1000, 16), jnp.float32)
        tbl_32 = 0.05 * jax.random.normal(jax.random.fold_in(_tk, 500 + 32), (12500, 16), jnp.float32)
        tbl_33 = 0.05 * jax.random.normal(jax.random.fold_in(_tk, 500 + 33), (1000, 16), jnp.float32)
        tbl_34 = 0.05 * jax.random.normal(jax.random.fold_in(_tk, 500 + 34), (1000, 16), jnp.float32)
        tbl_35 = 0.05 * jax.random.normal(jax.random.fold_in(_tk, 500 + 35), (12500, 16), jnp.float32)
        tbl_36 = 0.05 * jax.random.normal(jax.random.fold_in(_tk, 500 + 36), (125000, 16), jnp.float32)
        tbl_37 = 0.05 * jax.random.normal(jax.random.fold_in(_tk, 500 + 37), (1250, 16), jnp.float32)
        tbl_38 = 0.05 * jax.random.normal(jax.random.fold_in(_tk, 500 + 38), (1250, 16), jnp.float32)
        _rk = jax.random.fold_in(_tk, 7)
        W_top1 = 0.05 * jax.random.normal(jax.random.fold_in(_tk, 801), (400, 512), jnp.float32)
        W_top2 = 0.0441942 * jax.random.normal(jax.random.fold_in(_tk, 802), (512, 256), jnp.float32)
        W_top3 = 0.0625 * jax.random.normal(jax.random.fold_in(_tk, 803), (256, 1), jnp.float32)
        b_top1 = jnp.zeros((512,), jnp.float32)
        b_top2 = jnp.zeros((256,), jnp.float32)
        return (dense_ctx, ids, tbl_0, tbl_1, tbl_2, tbl_3, tbl_4, tbl_5, tbl_6, tbl_7, tbl_8, tbl_9, tbl_10, tbl_11, tbl_12, tbl_13, tbl_14, tbl_15, tbl_16, tbl_17, tbl_18, tbl_19, tbl_20, tbl_21, tbl_22, tbl_23, tbl_24, tbl_25, tbl_26, tbl_27, tbl_28, tbl_29, tbl_30, tbl_31, tbl_32, tbl_33, tbl_34, tbl_35, tbl_36, tbl_37, tbl_38, W_top1, b_top1, W_top2, b_top2, W_top3)
    dense_ctx, ids, tbl_0, tbl_1, tbl_2, tbl_3, tbl_4, tbl_5, tbl_6, tbl_7, tbl_8, tbl_9, tbl_10, tbl_11, tbl_12, tbl_13, tbl_14, tbl_15, tbl_16, tbl_17, tbl_18, tbl_19, tbl_20, tbl_21, tbl_22, tbl_23, tbl_24, tbl_25, tbl_26, tbl_27, tbl_28, tbl_29, tbl_30, tbl_31, tbl_32, tbl_33, tbl_34, tbl_35, tbl_36, tbl_37, tbl_38, W_top1, b_top1, W_top2, b_top2, W_top3 = _rec_inputs()

    def _L0_rec_setup():
        import jax, jax.numpy as jnp
        import numpy as np
        B, F0, D = (256, 39, 16)
        CROSS = [128, 128, 128]
        key = jax.random.key(seed)
        k0, k1, k2, k3 = jax.random.split(key, 4)
        inputs = jax.random.normal(k0, (B, F0, D), dtype=jnp.float32)
        f0 = jax.random.normal(k1, (F0 * F0, CROSS[0]), dtype=jnp.float32) * 0.05
        f1 = jax.random.normal(k2, (CROSS[0] * F0, CROSS[1]), dtype=jnp.float32) * 0.05
        f2 = jax.random.normal(k3, (CROSS[1] * F0, CROSS[2]), dtype=jnp.float32) * 0.05
        return {'inputs': inputs, 'f0': f0, 'f1': f1, 'f2': f2}
    _L0_rec_all = _L0_rec_setup()
    _L0_rec_in = {k: v for k, v in _L0_rec_all.items() if k in ('f0', 'f1', 'f2')}
    del _L0_rec_all
    return {'dense_ctx': dense_ctx, 'ids': ids, 'tbl_0': tbl_0, 'tbl_1': tbl_1, 'tbl_2': tbl_2, 'tbl_3': tbl_3, 'tbl_4': tbl_4, 'tbl_5': tbl_5, 'tbl_6': tbl_6, 'tbl_7': tbl_7, 'tbl_8': tbl_8, 'tbl_9': tbl_9, 'tbl_10': tbl_10, 'tbl_11': tbl_11, 'tbl_12': tbl_12, 'tbl_13': tbl_13, 'tbl_14': tbl_14, 'tbl_15': tbl_15, 'tbl_16': tbl_16, 'tbl_17': tbl_17, 'tbl_18': tbl_18, 'tbl_19': tbl_19, 'tbl_20': tbl_20, 'tbl_21': tbl_21, 'tbl_22': tbl_22, 'tbl_23': tbl_23, 'tbl_24': tbl_24, 'tbl_25': tbl_25, 'tbl_26': tbl_26, 'tbl_27': tbl_27, 'tbl_28': tbl_28, 'tbl_29': tbl_29, 'tbl_30': tbl_30, 'tbl_31': tbl_31, 'tbl_32': tbl_32, 'tbl_33': tbl_33, 'tbl_34': tbl_34, 'tbl_35': tbl_35, 'tbl_36': tbl_36, 'tbl_37': tbl_37, 'tbl_38': tbl_38, 'W_top1': W_top1, 'b_top1': b_top1, 'W_top2': W_top2, 'b_top2': b_top2, 'W_top3': W_top3, 'L0_rec_f0': _L0_rec_in['f0'], 'L0_rec_f1': _L0_rec_in['f1'], 'L0_rec_f2': _L0_rec_in['f2']}

def reference(dense_ctx, ids, tbl_0, tbl_1, tbl_2, tbl_3, tbl_4, tbl_5, tbl_6, tbl_7, tbl_8, tbl_9, tbl_10, tbl_11, tbl_12, tbl_13, tbl_14, tbl_15, tbl_16, tbl_17, tbl_18, tbl_19, tbl_20, tbl_21, tbl_22, tbl_23, tbl_24, tbl_25, tbl_26, tbl_27, tbl_28, tbl_29, tbl_30, tbl_31, tbl_32, tbl_33, tbl_34, tbl_35, tbl_36, tbl_37, tbl_38, W_top1, b_top1, W_top2, b_top2, W_top3, L0_rec_f0, L0_rec_f1, L0_rec_f2):
    import jax
    import jax.numpy as jnp

    def _L0_rec_ref(inputs, f0, f1, f2):
        import jax, jax.numpy as jnp
        import numpy as np
        B, F0, D = (256, 39, 16)
        CROSS = [128, 128, 128]
        filters = [f0, f1, f2]
        x0 = inputs
        xk = inputs
        outs = []
        for W in filters:
            b, f, d = x0.shape
            g = xk.shape[1]
            z = jnp.einsum('bfd,bgd->bfgd', x0, xk).reshape(b, f * g, d)
            cur = jnp.einsum('bpd,pm->bmd', z, W)
            outs.append(cur)
            xk = cur
        result = jnp.concatenate(outs, axis=1)
        return jnp.sum(result, axis=-1)
    e = jnp.stack([tbl_0[ids[:, 0]], tbl_1[ids[:, 1]], tbl_2[ids[:, 2]], tbl_3[ids[:, 3]], tbl_4[ids[:, 4]], tbl_5[ids[:, 5]], tbl_6[ids[:, 6]], tbl_7[ids[:, 7]], tbl_8[ids[:, 8]], tbl_9[ids[:, 9]], tbl_10[ids[:, 10]], tbl_11[ids[:, 11]], tbl_12[ids[:, 12]], tbl_13[ids[:, 13]], tbl_14[ids[:, 14]], tbl_15[ids[:, 15]], tbl_16[ids[:, 16]], tbl_17[ids[:, 17]], tbl_18[ids[:, 18]], tbl_19[ids[:, 19]], tbl_20[ids[:, 20]], tbl_21[ids[:, 21]], tbl_22[ids[:, 22]], tbl_23[ids[:, 23]], tbl_24[ids[:, 24]], tbl_25[ids[:, 25]], tbl_26[ids[:, 26]], tbl_27[ids[:, 27]], tbl_28[ids[:, 28]], tbl_29[ids[:, 29]], tbl_30[ids[:, 30]], tbl_31[ids[:, 31]], tbl_32[ids[:, 32]], tbl_33[ids[:, 33]], tbl_34[ids[:, 34]], tbl_35[ids[:, 35]], tbl_36[ids[:, 36]], tbl_37[ids[:, 37]], tbl_38[ids[:, 38]]], axis=1)
    z = _L0_rec_ref(e, L0_rec_f0, L0_rec_f1, L0_rec_f2)
    z = z.reshape(z.shape[0], -1)
    h = jnp.concatenate([z, dense_ctx], axis=1)
    h = jnp.maximum(h @ W_top1 + b_top1, 0.0)
    h = jnp.maximum(h @ W_top2 + b_top2, 0.0)
    y = h @ W_top3
    return y

_drawn_inputs = setup_inputs


def setup_inputs(seed=0):
    import zlib

    import numpy as np

    out = dict(_drawn_inputs(seed))
    spreads = {'b_top1': (0.0, 0.54), 'b_top2': (0.0, 0.1)}
    factors = {'tbl_0': 4.618,
     'tbl_1': 4.777,
     'tbl_2': 4.523,
     'tbl_3': 4.859,
     'tbl_4': 4.99,
     'tbl_5': 4.913,
     'tbl_6': 4.694,
     'tbl_7': 4.566,
     'tbl_8': 4.938,
     'tbl_9': 4.416,
     'tbl_10': 4.877,
     'tbl_11': 4.571,
     'tbl_12': 4.451,
     'tbl_13': 4.38,
     'tbl_14': 4.612,
     'tbl_15': 4.658,
     'tbl_16': 5.121,
     'tbl_17': 4.613,
     'tbl_18': 4.981,
     'tbl_19': 4.931,
     'tbl_20': 4.953,
     'tbl_21': 4.69,
     'tbl_22': 4.927,
     'tbl_23': 4.96,
     'tbl_24': 4.603,
     'tbl_25': 4.453,
     'tbl_26': 4.864,
     'tbl_27': 4.98,
     'tbl_28': 4.895,
     'tbl_29': 4.695,
     'tbl_30': 4.819,
     'tbl_31': 4.215,
     'tbl_32': 4.931,
     'tbl_33': 4.709,
     'tbl_34': 4.959,
     'tbl_35': 4.588,
     'tbl_36': 4.921,
     'tbl_37': 4.862,
     'tbl_38': 4.897,
     'L0_rec_f1': 5.063,
     'L0_rec_f2': 8.0}
    for name, (base, spread) in spreads.items():
        noise = np.random.default_rng([zlib.crc32(name.encode()), seed]).standard_normal(out[name].shape)
        drawn = base * np.exp(spread * noise) if base else spread * noise
        out[name] = jnp.asarray(drawn.astype(out[name].dtype))
    for name, factor in factors.items():
        out[name] = (out[name] * factor).astype(out[name].dtype)
    return out
```

```python
from contextlib import ExitStack

import numpy as np

import concourse.bass as bass
from concourse import mybir

F32 = mybir.dt.float32
F32R = mybir.dt.float32r
U32 = mybir.dt.uint32
ALU = mybir.AluOpType
ACT = mybir.ActivationFunctionType
AX_X = mybir.AxisListType.X

P = 128
B, F, D, G = 1024, 39, 16, 128
H1, H2 = 512, 256
DENSE = 16
TB = P // D
TILES = 4
GCOLS = TILES * P
BATCH = P
GROUPS = BATCH * D // GCOLS
STEPS = GROUPS * TILES
NBATCH = B // BATCH
NGROUP = GROUPS * NBATCH

SHIFTS = F // 2 + 1
SPT = P // F
KT = -(-SHIFTS // SPT)
KR = SPT * F
FX = F + 1
LOW = 64
HL = LOW + FX

FB = 4
BANKS = -(-F // FB)
RING = 4
ACT_BANKS = (1, 4, 6, 8)
NA = len(ACT_BANKS)
DVE_BANKS = tuple(q for q in range(BANKS) if q not in ACT_BANKS)
MACS = sum(min(FB, F - FB * q) for q in DVE_BANKS)
CHAINS = 2
TERMS = NA * FB + CHAINS
PARTS = NA * FB
W1_CHUNKS = 3
SEL_BANK, X1_BANK, S3_BANK, MISC_BANK = 4, 5, 6, 7
GATHERS_PER_STEP = 4
TREE = ((0, 9, 9), (0, 4, 4), (0, 2, 2), (0, 1, 1))


def selectors():
    sel = np.zeros((HL, 1 + KT, KR), np.float32)
    for i in range(SPT):
        for f in range(F):
            for low in (0, LOW):
                sel[low + f, 0, i * F + f] = 1
                for k in range(KT):
                    if SPT * k + i < SHIFTS:
                        sel[low + (f + SPT * k + i) % F, 1 + k, i * F + f] = 1
    both = np.zeros((HL, FX), np.float32)
    for f in range(FX):
        both[f, f] = 1
        if f < F:
            both[LOW + f, f] = 1
    mask = (np.arange(P)[:, None] // D == np.arange(TB)[None, :]).astype(np.float32)
    return sel.reshape(HL, -1), both, mask, np.eye(P, dtype=np.float32)


def pair_rows():
    s = np.arange(SHIFTS)[:, None]
    f = np.arange(F)[None, :]
    g = (f + s) % F
    return (f * F + g).reshape(-1), (g * F + f)[1:].reshape(-1)


def cin_tower(nc, dense_ctx, ids, tables, w_top1, b_top1, w_top2, b_top2, w_top3,
              w0_pair, w0_mirror, f1, f2, c_sel, c_both, c_mask, c_eye, out):
    with ExitStack() as ctx:
        def sb(name, shape, dt=F32):
            return ctx.enter_context(nc.sbuf_tensor(name, shape, dt))

        def sem(name):
            return ctx.enter_context(nc.semaphore(name))

        w1_high = sb("w1_high", [P, F * G], F32R)
        w1_low = sb("w1_low", [P, F * G], F32R)
        w2 = sb("w2", [P, F, G])
        w0_a = sb("w0_a", [KR, KT, G])
        w0_b = sb("w0_b", [KR, KT, G])
        sel_raw = sb("sel_raw", [HL, (1 + KT) * KR])
        sel = sb("sel", [HL, 1 + KT, KR], F32R)
        both_raw = sb("both_raw", [HL, FX])
        both = sb("both", [HL, FX], F32R)
        mask = sb("mask", [P, TB])
        eye = sb("eye", [P, P])
        ids_now = sb("ids_now", [P, F], U32)
        x0_rows = sb("x0_rows", [P, F, D])
        x0_parts = sb("x0_parts", [P, D, HL], F32R)
        x0_cols = sb("x0_cols", [HL, BATCH * D], F32R)
        x0_copy = sb("x0_copy", [KR, GCOLS])
        pairs = sb("pairs", [KR, KT, GCOLS])
        x1_high = sb("x1_high", [P, 2, GCOLS], F32R)
        x1_low = sb("x1_low", [P, 2, GCOLS], F32R)
        x0_scal = sb("x0_scal", [P, 2, TILES, FX])
        x0_diag = sb("x0_diag", [P, 2, TB, FX])
        terms = sb("terms", [P, 2, TERMS, G])
        x2 = sb("x2", [P, 2, G])
        s3 = sb("s3", [P, FX, BATCH])
        r1 = sb("r1", [P, B])
        r2 = sb("r2", [P, B])
        r3 = sb("r3", [P, B])
        wt1 = sb("wt1", [P, 3, H1])
        wt1_dense = sb("wt1_dense", [DENSE, H1])
        wt2 = sb("wt2", [P, H1 // P, H2])
        wt3 = sb("wt3", [P, H2 // P])
        bt1 = sb("bt1", [P, H1 // P])
        bt2 = sb("bt2", [P, H2 // P])
        dense_rows = sb("dense_rows", [P, NBATCH, DENSE])
        dense_t = sb("dense_t", [DENSE, B])
        y_row = sb("y_row", [1, B])
        w1_raw = s3[:, :, :].rearrange("p f b -> p (f b)")[:, 0:F * G]
        h1 = terms[:, :, :, :].rearrange("p a t g -> p (a t g)")[:, 0:2 * H1 // P * 512] \
            .rearrange("p (h c n) -> p h c n", h=2, c=H1 // P)
        h2 = [sb(f"h2_{h}", [P, H2 // P, 512]) for h in range(2)]

        ps = ctx.enter_context(nc.psum_tensor("ps", [P, 8, 512], F32))

        s_ids = sem("ids_loaded")
        s_const = sem("constants_loaded")
        s_w1 = [sem(f"w1_loaded{c}") for c in range(W1_CHUNKS)]
        s_w0 = sem("w0_loaded")
        s_w2 = sem("w2_loaded")
        s_top = sem("mlp_weights_loaded")
        s_gather = sem("rows_gathered")
        s_clear = sem("buffers_cleared")
        s_sel = sem("selectors_rounded")
        s_w1h = sem("w1_high_ready")
        s_w1l = sem("w1_low_ready")
        s_w0s = sem("w0_folded")
        s_parts = sem("x0_parts_ready")
        s_turn = sem("x0_transposed")
        s_cols = sem("x0_cols_stored")
        s_pick = sem("rows_picked")
        s_copy = sem("x0_copy_stored")
        s_pair = sem("pairs_ready")
        s_x1 = sem("x1_summed")
        s_x1h = sem("x1_high_ready")
        s_x1l = sem("x1_low_ready")
        s_r1 = sem("r1_ready")
        s_st = sem("scalars_turned")
        s_scal = sem("scalars_stored")
        s_y = sem("y_bank_ready")
        s_ya = sem("y_bank_scaled")
        s_mac = sem("macs_done")
        s_tree = sem("partial_adds")
        s_x2 = sem("x2_ready")
        s_diag = sem("x0_diag_ready")
        s_s3 = sem("s3_summed")
        s_s3e = sem("s3_stored")
        s_l3 = sem("r3_summed")
        s_r = sem("r2_r3_stored")
        s_den = sem("dense_turned")
        s_dene = sem("dense_stored")
        s_h1 = sem("h1_summed")
        s_h1e = sem("h1_stored")
        s_h2 = sem("h2_summed")
        s_h2e = sem("h2_stored")
        s_out = sem("y_summed")
        s_oute = sem("y_stored")
        s_done = sem("output_written")

        CREDIT_A, CREDIT_MAC, CREDIT_X2, CREDIT_S3, CREDIT_S3E, CREDIT_R = NA, MACS, 2, 2, 1, 1

        def banks_before(kind, n):
            t, q = divmod(n, BANKS)
            return t * len(kind) + sum(1 for k in kind if k < q)

        def macs_before(n):
            t, q = divmod(n, BANKS)
            return t * MACS + sum(min(FB, F - FB * k) for k in DVE_BANKS if k < q)

        def prologue_then_batches(eng, step, prologue, tail):
            prologue()
            for u in range(2):
                step(0, u, False)
            with eng.Fori(0, NBATCH - 1) as bt:
                for u in range(2, STEPS + 2):
                    step(bt, u, False)
            for u in range(2, STEPS):
                step(NBATCH - 1, u, True)
            tail(NBATCH - 1)

        block = ctx.enter_context(nc.Block())

        @block.sync
        def _(sp):
            sp.dma_start(ids_now[:, :], ids[0:BATCH, :].bitcast(U32)).then_inc(s_ids, 16)
            sp.dma_start(w0_a[:, :, :], w0_pair.rearrange("k r m -> r k m")).then_inc(s_w0, 16)
            sp.dma_start(w0_b[:, :, :], w0_mirror.rearrange("k r m -> r k m")).then_inc(s_w0, 16)
            f1_v = f1.rearrange("(f g) m -> g f m", g=G)
            n = F // W1_CHUNKS
            for c in range(W1_CHUNKS):
                sp.dma_start(w1_raw[:, c * n * G:(c + 1) * n * G].rearrange("p (f m) -> p f m", m=G),
                             f1_v[:, c * n:(c + 1) * n, :]).then_inc(s_w1[c], 16)
            sp.dma_start(w2[:, :, :], f2.rearrange("(f g) m -> g f m", g=G)).then_inc(s_w2, 16)
            with sp.Fori(0, NBATCH - 1) as bt:
                sp.wait_ge(s_gather, (bt + 1) * (16 * F))
                sp.dma_start(ids_now[:, :], ids[bass.ds((bt + 1) * BATCH, BATCH), :].bitcast(U32)) \
                    .then_inc(s_ids, 16)
            for h in range(2):
                sp.wait_ge(s_oute, h + 1)
                sp.dma_start(out.rearrange("b o -> o b")[:, h * 512:(h + 1) * 512],
                             y_row[:, h * 512:(h + 1) * 512]).then_inc(s_done, 16)
            sp.wait_ge(s_done, 32)

        @block.gpsimd
        def _(pool):
            pool.sem_inc(s_x2, CREDIT_X2)

            def gather(f):
                pool.indirect_dma_start(
                    out=x0_rows[:, f, :], out_offset=None, in_=tables[f],
                    in_offset=bass.IndirectOffsetOnAxis(ap=ids_now[:, f:f + 1], axis=0),
                ).then_inc(s_gather, 16)

            def prologue():
                pool.wait_ge(s_ids, 16)
                for f in range(F):
                    gather(f)

            def add_up(bt, u):
                t = terms[:, u % 2]
                pool.wait_ge(s_ya, bt * (STEPS * NA) + NA * (u + 1) + CREDIT_A)
                pool.wait_ge(s_mac, bt * (STEPS * MACS) + MACS * (u + 1) + CREDIT_MAC)
                for i, (to, at, n) in enumerate(TREE):
                    if i:
                        pool.wait_ge(s_tree, bt * (STEPS * len(TREE)) + len(TREE) * u + i)
                    nc.gpsimd.tensor_tensor(t[:, to:to + n], t[:, to:to + n], t[:, at:at + n],
                                            ALU.add).then_inc(s_tree, 1)
                pool.wait_ge(s_tree, bt * (STEPS * len(TREE)) + len(TREE) * (u + 1))
                pool.wait_ge(s_s3, bt * STEPS + u - 1 + CREDIT_S3)
                nc.gpsimd.tensor_tensor(x2[:, u % 2], t[:, 0], t[:, TERMS // 2 - 1],
                                        ALU.add).then_inc(s_x2, 1)

            def step(bt, u, last):
                first = GATHERS_PER_STEP * (u - 2)
                gathers = () if last or u < 2 else range(first, min(first + GATHERS_PER_STEP, F))
                if gathers and u == 2:
                    pool.wait_ge(s_ids, (bt + 2) * 16)
                    pool.wait_ge(s_parts, (bt + 1) * 2)
                add_up(bt, u)
                for f in gathers:
                    gather(f)

            prologue_then_batches(pool, step, prologue, lambda bt: None)

        @block.tensor
        def _(pe):
            pe.sem_inc(s_s3, CREDIT_S3)

            def turn(bt, r):
                pe.wait_ge(s_parts, (bt + 1) * 2)
                if r == 0:
                    pe.wait_ge(s_scal, bt * GROUPS)
                else:
                    pe.wait_ge(s_cols, bt * 4 + r)
                for i in range(4):
                    mm = nc.tensor.transpose(ps[0:HL, MISC_BANK, i * P:(i + 1) * P],
                                             x0_parts[:, 4 * r + i, :].bitcast(F32), eye[:, :])
                mm.then_inc(s_turn, 1)

            def pick(gf, j, k):
                if k == 0 and j % GROUPS == 0:
                    pe.wait_ge(s_cols, gf + 4)
                if k == 1:
                    pe.wait_ge(s_copy, gf + 1)
                else:
                    pe.wait_ge(s_pair, gf * KT + max(k - 1, 0))
                nc.tensor.matmul(ps[0:KR, SEL_BANK, :], sel[:, k, :],
                                 x0_cols[:, j % GROUPS * GCOLS:(j % GROUPS + 1) * GCOLS],
                                 start=True, stop=True).then_inc(s_pick, 1)

            def turn_scalars(gf, j, bt):
                pe.wait_ge(s_scal, gf)
                if bt is not None:
                    pe.wait_ge(s_r, bt * 2 + CREDIT_R)
                for t in range(TILES):
                    at = (j % GROUPS * TILES + t) * P
                    mm = nc.tensor.matmul(ps[:, MISC_BANK, t * FX:(t + 1) * FX], x0_cols[:, at:at + P],
                                          both[:, :], start=True, stop=True)
                mm.then_inc(s_st, 1)

            def cin1(gf, k):
                if k == 0:
                    pe.wait_ge(s_r1, gf)
                pe.wait_ge(s_pair, gf * KT + k + 1)
                mm = nc.tensor.matmul(ps[:, X1_BANK, :], w0_a[:, k, :], pairs[:, k, :],
                                      start=(k == 0), stop=(k == KT - 1))
                if k == KT - 1:
                    mm.then_inc(s_x1, 1)

            def cin2(bt, u, q):
                n = BANKS * u + q
                old = n - RING
                if old % BANKS in ACT_BANKS:
                    pe.wait_ge(s_ya, bt * (STEPS * NA) + banks_before(ACT_BANKS, old + 1) + CREDIT_A)
                else:
                    pe.wait_ge(s_mac, bt * (STEPS * MACS) + macs_before(old + 1) + CREDIT_MAC)
                if u % TILES == 0 and q == 0:
                    pe.wait_ge(s_x1h, bt * GROUPS + u // TILES + 1)
                    pe.wait_ge(s_x1l, bt * GROUPS + u // TILES + 1)
                par, at = u // TILES % 2, u % TILES * P
                width = min(FB, F - FB * q) * G
                y = ps[:, n % RING, 0:width]
                high = w1_high[:, q * FB * G:q * FB * G + width]
                low = w1_low[:, q * FB * G:q * FB * G + width]
                nc.tensor.matmul(y, x1_high[:, par, at:at + P], high, start=True, stop=False)
                nc.tensor.matmul(y, x1_high[:, par, at:at + P], low, start=False, stop=False)
                nc.tensor.matmul(y, x1_low[:, par, at:at + P], high, start=False, stop=True) \
                    .then_inc(s_y, 1)

            def sum_s3(bt, u):
                pe.wait_ge(s_x2, bt * STEPS + u - 1 + CREDIT_X2)
                pe.wait_ge(s_diag, bt * STEPS + u - 1)
                pe.wait_ge(s_s3e, bt * STEPS + u - 2 + CREDIT_S3E)
                nc.tensor.matmul(ps[:, S3_BANK, 0:TB * FX], x2[:, u % 2, :],
                                 x0_diag[:, u % 2].rearrange("p b f -> p (b f)"),
                                 start=True, stop=True).then_inc(s_s3, 1)

            def cin3(bt, lo, hi, scalars):
                if lo == 0:
                    pe.wait_ge(s_s3e, bt * STEPS + STEPS + CREDIT_S3E)
                    pe.wait_ge(s_scal, scalars)
                for f in range(lo, hi):
                    mm = nc.tensor.matmul(ps[:, MISC_BANK, 0:BATCH], w2[:, f, :], s3[:, f, :],
                                          start=(f == 0), stop=(f == F - 1))
                if hi == F:
                    mm.then_inc(s_l3, 1)

            def prologue():
                pe.wait_ge(s_const, 16 * 4)
                pe.wait_ge(s_sel, 2)
                pe.wait_ge(s_top, 16 * 7)
                for c in range(NBATCH // 4):
                    for i in range(4):
                        mm = nc.tensor.transpose(ps[0:DENSE, c, i * P:(i + 1) * P],
                                                 dense_rows[:, 4 * c + i, :], eye[:, :])
                    mm.then_inc(s_den, 1)
                for r in range(4):
                    turn(0, r)
                pick(0, 0, 0)
                turn_scalars(0, 0, None)
                for k in range(KT):
                    pick(0, 0, k + 1)
                pe.wait_ge(s_w0s, 1)
                for k in range(KT):
                    cin1(0, k)
                pe.wait_ge(s_w1h, W1_CHUNKS)
                pe.wait_ge(s_w1l, W1_CHUNKS)
                pe.wait_ge(s_dene, NBATCH // 4)
                pe.wait_ge(s_w2, 16)

            def step(bt, u, last):
                tile, j = u % TILES, u // TILES + 1
                front = not (last and j == GROUPS)
                gf = bt * GROUPS + j
                for q in range(BANKS):
                    cin2(bt, u, q)
                    if q == 4 and u >= 2:
                        sum_s3(bt, u)
                    if front and tile == 0:
                        if j == GROUPS and q in (1, 3, 5, 7):
                            turn(bt + 1, q // 2)
                        if q == 9:
                            pick(gf, j, 0)
                    if front and tile == 1:
                        if q == 0:
                            turn_scalars(gf, j, bt if j == 2 else None)
                        if q % 2:
                            pick(gf, j, q // 2 + 1)
                    if front and tile == 2:
                        if q in (1, 3):
                            pick(gf, j, q // 2 + 6)
                        if q in (5, 7, 9):
                            cin1(gf, (q - 5) // 2)
                    if front and tile == 3 and q in (0, 2, 4, 5):
                        cin1(gf, 3 + (0, 2, 4, 5).index(q))
                    if u == STEPS + 1 and q >= 6:
                        cin3(bt, (q - 6) * 10, min((q - 5) * 10, F), bt * GROUPS + GROUPS + 2)

            def tail(bt):
                sum_s3(bt, STEPS)
                sum_s3(bt, STEPS + 1)
                cin3(bt, 0, F, NGROUP)
                pe.wait_ge(s_r, 2 * NBATCH + CREDIT_R)
                pe.wait_ge(s_r1, NGROUP)
                for h in range(2):
                    cols = slice(h * 512, (h + 1) * 512)
                    for c in range(H1 // P):
                        for k, x in enumerate((r1, r2, r3)):
                            nc.tensor.matmul(ps[:, 4 * h + c, :], wt1[:, k, c * P:(c + 1) * P], x[:, cols],
                                             start=(k == 0), stop=False)
                        nc.tensor.matmul(ps[:, 4 * h + c, :], wt1_dense[:, c * P:(c + 1) * P],
                                         dense_t[:, cols], start=False, stop=True).then_inc(s_h1, 1)
                for h in range(2):
                    pe.wait_ge(s_h1e, 4 * h + 4)
                    for c in range(H2 // P):
                        for k in range(H1 // P):
                            mm = nc.tensor.matmul(ps[:, 2 * h + c, :], wt2[:, k, c * P:(c + 1) * P],
                                                  h1[:, h, k, :], start=(k == 0), stop=(k == H1 // P - 1))
                        mm.then_inc(s_h2, 1)
                for h in range(2):
                    pe.wait_ge(s_h2e, 2 * h + 2)
                    for k in range(H2 // P):
                        mm = nc.tensor.matmul(ps[0:1, 4 + h, :], wt3[:, k:k + 1], h2[h][:, k, :],
                                              start=(k == 0), stop=(k == H2 // P - 1))
                    mm.then_inc(s_out, 1)

            prologue_then_batches(pe, step, prologue, tail)

        @block.scalar
        def _(act):
            act.dma_start(eye[:, :], c_eye[:, :]).then_inc(s_const, 16)
            act.dma_start(sel_raw[:, :], c_sel[:, :]).then_inc(s_const, 16)
            act.dma_start(both_raw[:, :], c_both[:, :]).then_inc(s_const, 16)
            act.dma_start(mask[:, :], c_mask[:, :]).then_inc(s_const, 16)
            act.dma_start(wt1[:, :, :], w_top1[0:3 * P, :].rearrange("(k p) n -> p k n", p=P)) \
                .then_inc(s_top, 16)
            act.dma_start(wt1_dense[:, :], w_top1[3 * P:3 * P + DENSE, :]).then_inc(s_top, 16)
            act.dma_start(wt2[:, :, :], w_top2.rearrange("(k p) n -> p k n", p=P)).then_inc(s_top, 16)
            act.dma_start(wt3[:, :], w_top3[:, :]).then_inc(s_top, 16)
            act.dma_start(bt1[:, :], b_top1[:, :]).then_inc(s_top, 16)
            act.dma_start(bt2[:, :], b_top2[:, :]).then_inc(s_top, 16)
            act.dma_start(dense_rows[:, :, :], dense_ctx.rearrange("(c p) k -> p c k", p=P)) \
                .then_inc(s_top, 16)
            act.sem_inc(s_ya, CREDIT_A)
            act.sem_inc(s_s3e, CREDIT_S3E)
            act.sem_inc(s_r, CREDIT_R)

            def store_cols(bt, r):
                act.wait_ge(s_turn, bt * 4 + r + 1)
                nc.scalar.activation(
                    x0_cols[:, :].rearrange("k (b d) -> k d b", d=D)[:, 4 * r:4 * r + 4, :],
                    ps[0:HL, MISC_BANK, :].rearrange("k (d b) -> k d b", d=4), ACT.Copy).then_inc(s_cols, 1)

            def store_copy(gf):
                act.wait_ge(s_pick, gf * (1 + KT) + 1)
                nc.scalar.activation(x0_copy[:, :], ps[0:KR, SEL_BANK, :], ACT.Copy).then_inc(s_copy, 1)

            def store_scalars(gf, j, guard):
                act.wait_ge(s_st, gf + 1)
                if guard:
                    act.wait_ge(s_diag, (gf - 1) * TILES)
                nc.scalar.activation(x0_scal[:, j % 2].rearrange("p t f -> p (t f)"),
                                     ps[:, MISC_BANK, 0:TILES * FX], ACT.Copy).then_inc(s_scal, 1)

            def store_x1(gf, j):
                act.wait_ge(s_x1, gf + 1)
                nc.scalar.activation(x1_high[:, j % 2, :], ps[:, X1_BANK, :], ACT.Copy).then_inc(s_x1h, 1)

            def scale(bt, u, q):
                if q == ACT_BANKS[0]:
                    act.wait_ge(s_x2, bt * STEPS + u - 1 + CREDIT_X2)
                    if u % TILES == 0:
                        act.wait_ge(s_scal, bt * GROUPS + u // TILES + 1)
                act.wait_ge(s_y, bt * (STEPS * BANKS) + BANKS * u + q + 1)
                for i in range(FB):
                    f = FB * q + i
                    op = nc.scalar.activation(
                        terms[:, u % 2, FB * ACT_BANKS.index(q) + i, :],
                        ps[:, (BANKS * u + q) % RING, i * G:(i + 1) * G], ACT.Copy,
                        scale=x0_scal[:, u // TILES % 2, u % TILES, f:f + 1])
                op.then_inc(s_ya, 1)

            def store_s3(bt, u):
                if u == 2:
                    act.wait_ge(s_r, bt * 2 + CREDIT_R)
                act.wait_ge(s_s3, bt * STEPS + u - 1 + CREDIT_S3)
                at = (u - 2) * TB
                nc.scalar.activation(s3[:, :, at:at + TB],
                                     ps[:, S3_BANK, 0:TB * FX].rearrange("p (b f) -> p f b", f=FX),
                                     ACT.Copy).then_inc(s_s3e, 1)

            def store_r(bt):
                act.wait_ge(s_s3e, bt * STEPS + STEPS + CREDIT_S3E)
                nc.scalar.activation(r2[:, bass.ds(bt * BATCH, BATCH)], s3[:, F, :], ACT.Copy).then_inc(s_r, 1)
                act.wait_ge(s_l3, bt + 1)
                nc.scalar.activation(r3[:, bass.ds(bt * BATCH, BATCH)], ps[:, MISC_BANK, 0:BATCH],
                                     ACT.Copy).then_inc(s_r, 1)

            def prologue():
                n = F // W1_CHUNKS * G
                for c in range(W1_CHUNKS):
                    act.wait_ge(s_w1[c], 16)
                    nc.scalar.activation(w1_high[:, c * n:(c + 1) * n], w1_raw[:, c * n:(c + 1) * n],
                                         ACT.Copy).then_inc(s_w1h, 1)
                for c in range(NBATCH // 4):
                    act.wait_ge(s_den, c + 1)
                    nc.scalar.activation(dense_t[:, c * 512:(c + 1) * 512], ps[0:DENSE, c, :],
                                         ACT.Copy).then_inc(s_dene, 1)
                for r in range(4):
                    store_cols(0, r)
                store_copy(0)
                store_scalars(0, 0, False)
                store_x1(0, 0)

            def step(bt, u, last):
                tile, j = u % TILES, u // TILES + 1
                front = not (last and j == GROUPS)
                gf = bt * GROUPS + j
                for q in range(BANKS):
                    if q in ACT_BANKS:
                        scale(bt, u, q)
                    if q == 5 and u >= 2:
                        store_s3(bt, u)
                    if front and tile == 0:
                        if j == GROUPS and q in (2, 4, 6, 8):
                            store_cols(bt + 1, q // 2 - 1)
                        if q == 9:
                            store_copy(gf)
                    if front and tile == 1 and q == 0:
                        store_scalars(gf, j, True)
                    if front and tile == 3 and q == 6:
                        store_x1(gf, j)
                if u == STEPS + 1:
                    store_r(bt)

            def tail(bt):
                store_s3(bt, STEPS)
                store_s3(bt, STEPS + 1)
                store_r(bt)
                for h in range(2):
                    for c in range(H1 // P):
                        act.wait_ge(s_h1, 4 * h + c + 1)
                        nc.scalar.activation(h1[:, h, c, :], ps[:, 4 * h + c, :], ACT.Relu,
                                             bias=bt1[:, c:c + 1]).then_inc(s_h1e, 1)
                for h in range(2):
                    for c in range(H2 // P):
                        act.wait_ge(s_h2, 2 * h + c + 1)
                        nc.scalar.activation(h2[h][:, c, :], ps[:, 2 * h + c, :], ACT.Relu,
                                             bias=bt2[:, c:c + 1]).then_inc(s_h2e, 1)
                for h in range(2):
                    act.wait_ge(s_out, h + 1)
                    nc.scalar.activation(y_row[:, h * 512:(h + 1) * 512], ps[0:1, 4 + h, :],
                                         ACT.Copy).then_inc(s_oute, 1)

            prologue_then_batches(act, step, prologue, tail)

        @block.vector
        def _(dve):
            dve.sem_inc(s_mac, CREDIT_MAC)

            def split_x0(bt):
                dve.wait_ge(s_gather, (bt + 1) * (16 * F))
                dve.wait_ge(s_turn, bt * 4)
                rows = x0_rows[:, :, :].rearrange("p f d -> p d f")
                nc.vector.tensor_copy(x0_parts[:, :, 0:F], rows).then_inc(s_parts, 1)
                dve.wait_ge(s_parts, bt * 2 + 1)
                nc.vector.tensor_tensor(x0_parts[:, :, LOW:LOW + F], rows, x0_parts[:, :, 0:F].bitcast(F32),
                                        ALU.subtract).then_inc(s_parts, 1)

            def multiply(gf, k):
                dve.wait_ge(s_pick, gf * (1 + KT) + k + 2)
                if k == 0:
                    dve.wait_ge(s_copy, gf + 1)
                    dve.wait_ge(s_x1, gf)
                nc.vector.tensor_tensor(pairs[:, k, :], ps[0:KR, SEL_BANK, :], x0_copy[:, :],
                                        ALU.mult).then_inc(s_pair, 1)

            def split_x1(gf, j):
                dve.wait_ge(s_x1h, gf + 1)
                nc.vector.tensor_tensor(x1_low[:, j % 2, :], ps[:, X1_BANK, :],
                                        x1_high[:, j % 2, :].bitcast(F32), ALU.subtract).then_inc(s_x1l, 1)
                nc.vector.tensor_reduce(r1[:, bass.ds(gf * (GCOLS // D), GCOLS // D)],
                                        ps[:, X1_BANK, :].rearrange("p (b d) -> p b d", d=D),
                                        AX_X, ALU.add).then_inc(s_r1, 1)

            def mac(bt, u, q):
                if q == DVE_BANKS[0]:
                    dve.wait_ge(s_x2, bt * STEPS + u - 1 + CREDIT_X2)
                    if u % TILES == 0:
                        dve.wait_ge(s_scal, bt * GROUPS + u // TILES + 1)
                dve.wait_ge(s_y, bt * (STEPS * BANKS) + BANKS * u + q + 1)
                done = macs_before(q)
                for i in range(min(FB, F - FB * q)):
                    f, n = FB * q + i, done + i
                    acc = terms[:, u % 2, PARTS + n % CHAINS, :]
                    y = ps[:, (BANKS * u + q) % RING, i * G:(i + 1) * G]
                    x0 = x0_scal[:, u // TILES % 2, u % TILES, f:f + 1]
                    if n < CHAINS:
                        nc.vector.tensor_scalar(acc, y, x0, None, ALU.mult).then_inc(s_mac, 1)
                        continue
                    dve.wait_ge(s_mac, bt * (STEPS * MACS) + MACS * u + n - CHAINS + 1 + CREDIT_MAC)
                    nc.vector.scalar_tensor_tensor(out=acc, in0=y, scalar=x0, in1=acc, op0=ALU.mult,
                                                   op1=ALU.add).then_inc(s_mac, 1)

            def diagonal(bt, u):
                dve.wait_ge(s_s3, bt * STEPS + u - 2 + CREDIT_S3)
                t = u - 1
                nc.vector.tensor_tensor(
                    x0_diag[:, t % 2],
                    x0_scal[:, t // TILES % 2, t % TILES, :].unsqueeze(1).to_broadcast([P, TB, FX]),
                    mask[:, :].unsqueeze(2).to_broadcast([P, TB, FX]), ALU.mult).then_inc(s_diag, 1)

            def prologue():
                nc.vector.memset(x0_parts[:, :, :].bitcast(F32), 0.0).then_inc(s_clear, 1)
                dve.wait_ge(s_clear, 1)
                nc.vector.memset(x0_parts[:, :, F:FX].bitcast(F32), 1.0).then_inc(s_clear, 1)
                dve.wait_ge(s_const, 16 * 4)
                nc.vector.tensor_copy(sel[:, :, :].rearrange("k a b -> k (a b)"), sel_raw[:, :]) \
                    .then_inc(s_sel, 1)
                nc.vector.tensor_copy(both[:, :], both_raw[:, :]).then_inc(s_sel, 1)
                dve.wait_ge(s_w0, 32)
                nc.vector.tensor_tensor(w0_a[:, :, :], w0_a[:, :, :], w0_b[:, :, :], ALU.add) \
                    .then_inc(s_w0s, 1)
                n = F // W1_CHUNKS * G
                for c in range(W1_CHUNKS):
                    dve.wait_ge(s_w1h, c + 1)
                    nc.vector.tensor_tensor(w1_low[:, c * n:(c + 1) * n], w1_raw[:, c * n:(c + 1) * n],
                                            w1_high[:, c * n:(c + 1) * n].bitcast(F32), ALU.subtract) \
                        .then_inc(s_w1l, 1)
                dve.wait_ge(s_clear, 2)
                split_x0(0)
                for k in range(KT):
                    multiply(0, k)
                split_x1(0, 0)

            def step(bt, u, last):
                tile, j = u % TILES, u // TILES + 1
                front = not (last and j == GROUPS)
                gf = bt * GROUPS + j
                if front and tile == 0 and j == GROUPS:
                    split_x0(bt + 1)
                for q in range(BANKS):
                    if q in DVE_BANKS:
                        mac(bt, u, q)
                    if q == 2 and u >= 1:
                        diagonal(bt, u)
                    if front and tile == 1 and q in (2, 4, 6, 8):
                        multiply(gf, q // 2 - 1)
                    if front and tile == 2 and q in (0, 2, 4):
                        multiply(gf, 4 + q // 2)
                    if front and tile == 3 and q == 7:
                        split_x1(gf, j)

            prologue_then_batches(dve, step, prologue, lambda bt: diagonal(bt, STEPS))


TOP = ("W_top1", "b_top1", "W_top2", "b_top2", "W_top3")


def kernel(**inputs):
    import concourse.bacc as bacc
    from concourse.bass_utils import run_bass_kernel_spmd

    rows, mirror = pair_rows()
    f0 = np.asarray(inputs["L0_rec_f0"])
    w0_pair = np.zeros((KT * KR, G), f0.dtype)
    w0_pair[:SHIFTS * F] = f0[rows]
    w0_mirror = np.zeros((KT * KR, G), f0.dtype)
    w0_mirror[F:SHIFTS * F] = f0[mirror]
    c_sel, c_both, c_mask, c_eye = selectors()
    named = {"dense_ctx": inputs["dense_ctx"], "ids": inputs["ids"]}
    named |= {f"tbl_{f}": inputs[f"tbl_{f}"] for f in range(F)}
    named |= {name: inputs[name] for name in TOP}
    for name in ("b_top1", "b_top2", "W_top3"):
        named[name] = np.asarray(inputs[name]).reshape(-1, P).T
    named |= {"w0_pair": w0_pair.reshape(KT, KR, G), "w0_mirror": w0_mirror.reshape(KT, KR, G),
              "f1": inputs["L0_rec_f1"], "f2": inputs["L0_rec_f2"],
              "c_sel": c_sel, "c_both": c_both, "c_mask": c_mask, "c_eye": c_eye}
    nc = bacc.Bacc("TRN2", target_bir_lowering=False, num_devices=1)
    arrays, ap = {}, {}
    for name, x in named.items():
        a = np.ascontiguousarray(x)
        arrays["in_" + name] = a
        ap[name] = nc.dram_tensor("in_" + name, a.shape, mybir.dt.from_np(a.dtype), kind="ExternalInput").ap()
    out = nc.dram_tensor("out_y", (B, 1), F32, kind="ExternalOutput").ap()
    cin_tower(nc, ap["dense_ctx"], ap["ids"], [ap[f"tbl_{f}"] for f in range(F)],
              *[ap[name] for name in TOP], ap["w0_pair"], ap["w0_mirror"], ap["f1"], ap["f2"],
              ap["c_sel"], ap["c_both"], ap["c_mask"], ap["c_eye"], out)
    r = run_bass_kernel_spmd(nc, [arrays], core_ids=[0])
    return r.results[0]["out_y"]
```

```python
from contextlib import ExitStack

import numpy as np

import concourse.bass as bass
from concourse import mybir

F32 = mybir.dt.float32
F32R = mybir.dt.float32r
U32 = mybir.dt.uint32
ALU = mybir.AluOpType
ACT = mybir.ActivationFunctionType
AX_X = mybir.AxisListType.X

P = 128
B, F, D, G = 1024, 39, 16, 128
H1, H2 = 512, 256
DENSE = 16
TB = P // D
TILES = 4
GCOLS = TILES * P
BATCH = P
GROUPS = BATCH * D // GCOLS
STEPS = GROUPS * TILES
NBATCH = B // BATCH
NGROUP = GROUPS * NBATCH

SHIFTS = F // 2 + 1
SPT = P // F
KT = -(-SHIFTS // SPT)
KR = SPT * F
FX = F + 1
LOW = 64
HL = LOW + FX

FB = 4
BANKS = -(-F // FB)
RING = 4
ACT_BANKS = (0, 3, 5, 8)
NA = len(ACT_BANKS)
DVE_BANKS = tuple(q for q in range(BANKS) if q not in ACT_BANKS)
MACS = sum(min(FB, F - FB * q) for q in DVE_BANKS)
CHAINS = 2
TERMS = NA * FB
W1_CHUNKS = 3
SEL_BANKS, X1_BANK, MISC_BANK = (4, 5), 6, 7
TURNS = ((0, 0), (0, 2), (0, 6), (0, 8))
PICKS = ((0, 9), (1, 1), (1, 3), (1, 6), (1, 9), (2, 2), (2, 5), (2, 8))
SCALARS = (1, 0)
CIN1 = ((2, 1), (2, 4), (2, 7), (3, 0), (3, 1), (3, 3), (3, 5))
STORE_X1, SPLIT_X1 = (3, 6), (3, 7)
GATHERS_PER_STEP = 4
GATHER_END = 12
TREE = (8, 4, 2)


def selectors():
    sel = np.zeros((HL, 1 + KT, KR), np.float32)
    for i in range(SPT):
        for f in range(F):
            for low in (0, LOW):
                sel[low + f, 0, i * F + f] = 1
                for k in range(KT):
                    if SPT * k + i < SHIFTS:
                        sel[low + (f + SPT * k + i) % F, 1 + k, i * F + f] = 1
    both = np.zeros((HL, FX), np.float32)
    for f in range(FX):
        both[f, f] = 1
        if f < F:
            both[LOW + f, f] = 1
    mask = (np.arange(P)[:, None] // D == np.arange(TB)[None, :]).astype(np.float32)
    return sel.reshape(HL, -1), both, mask, np.eye(P, dtype=np.float32)


def pair_rows():
    s = np.arange(SHIFTS)[:, None]
    f = np.arange(F)[None, :]
    g = (f + s) % F
    return (f * F + g).reshape(-1), (g * F + f)[1:].reshape(-1)


def cin_tower(nc, dense_ctx, ids, tables, w_top1, b_top1, w_top2, b_top2, w_top3,
              w0_pair, w0_mirror, f1, f2, c_sel, c_both, c_mask, c_eye, out):
    with ExitStack() as ctx:
        def sb(name, shape, dt=F32):
            return ctx.enter_context(nc.sbuf_tensor(name, shape, dt))

        def sem(name):
            return ctx.enter_context(nc.semaphore(name))

        w1_high = sb("w1_high", [P, F * G], F32R)
        w1_low = sb("w1_low", [P, F * G], F32R)
        w2 = sb("w2", [P, F, G])
        w0_a = sb("w0_a", [KR, KT, G])
        w0_b = sb("w0_b", [KR, KT, G])
        sel_raw = sb("sel_raw", [HL, (1 + KT) * KR])
        sel = sb("sel", [HL, 1 + KT, KR], F32R)
        both_raw = sb("both_raw", [HL, FX])
        both = sb("both", [HL, FX], F32R)
        mask = sb("mask", [P, TB])
        eye = sb("eye", [P, P])
        ids_now = sb("ids_now", [P, F], U32)
        x0_rows = sb("x0_rows", [P, F, D])
        x0_parts = sb("x0_parts", [P, D, HL], F32R)
        x0_cols = sb("x0_cols", [HL, BATCH * D], F32R)
        x0_copy = sb("x0_copy", [KR, GCOLS])
        pairs = sb("pairs", [KR, KT, GCOLS])
        x1_high = sb("x1_high", [P, 2, GCOLS], F32R)
        x1_low = sb("x1_low", [P, 2, GCOLS], F32R)
        x0_scal = sb("x0_scal", [P, 2, TILES, FX])
        x0_diag = sb("x0_diag", [P, 2, TB, FX])
        terms = sb("terms", [P, 2, TERMS, G])
        x2 = sb("x2", [P, 2, G])
        s3 = sb("s3", [P, FX, BATCH])
        r1 = sb("r1", [P, B])
        r2 = sb("r2", [P, B])
        r3 = sb("r3", [P, B])
        wt1 = sb("wt1", [P, 3, H1])
        wt1_dense = sb("wt1_dense", [DENSE, H1])
        wt2 = sb("wt2", [P, H1 // P, H2])
        wt3 = sb("wt3", [P, H2 // P])
        bt1 = sb("bt1", [P, H1 // P])
        bt2 = sb("bt2", [P, H2 // P])
        dense_rows = sb("dense_rows", [P, NBATCH, DENSE])
        dense_t = sb("dense_t", [DENSE, B])
        y_row = sb("y_row", [1, B])
        w1_raw = s3[:, :, :].rearrange("p f b -> p (f b)")[:, 0:F * G]
        h1 = terms[:, :, :, :].rearrange("p a t g -> p (a t g)")[:, 0:2 * H1 // P * 512] \
            .rearrange("p (h c n) -> p h c n", h=2, c=H1 // P)
        h2 = [sb(f"h2_{h}", [P, H2 // P, 512]) for h in range(2)]

        ps = ctx.enter_context(nc.psum_tensor("ps", [P, 8, 512], F32))

        s_ids = sem("ids_loaded")
        s_const = sem("constants_loaded")
        s_w1 = [sem(f"w1_loaded{c}") for c in range(W1_CHUNKS)]
        s_w0 = sem("w0_loaded")
        s_w2 = sem("w2_loaded")
        s_top = sem("mlp_weights_loaded")
        s_gather = sem("rows_gathered")
        s_clear = sem("buffers_cleared")
        s_sel = sem("selectors_rounded")
        s_w1h = sem("w1_high_ready")
        s_w1l = sem("w1_low_ready")
        s_w0s = sem("w0_folded")
        s_parts = sem("x0_parts_ready")
        s_turn = sem("x0_transposed")
        s_cols = sem("x0_cols_stored")
        s_pick = sem("rows_picked")
        s_copy = sem("x0_copy_stored")
        s_pair = sem("pairs_ready")
        s_x1 = sem("x1_summed")
        s_x1h = sem("x1_high_ready")
        s_x1l = sem("x1_low_ready")
        s_r1 = sem("r1_ready")
        s_st = sem("scalars_turned")
        s_scal = sem("scalars_stored")
        s_y = sem("y_bank_ready")
        s_ya = sem("y_bank_scaled")
        s_mac = sem("macs_done")
        s_tree = sem("partial_adds")
        s_x2 = sem("x2_ready")
        s_diag = sem("x0_diag_ready")
        s_s3 = sem("s3_summed")
        s_s3e = sem("s3_stored")
        s_l3 = sem("r3_summed")
        s_r = sem("r2_r3_stored")
        s_den = sem("dense_turned")
        s_dene = sem("dense_stored")
        s_h1 = sem("h1_summed")
        s_h1e = sem("h1_stored")
        s_h2 = sem("h2_summed")
        s_h2e = sem("h2_stored")
        s_out = sem("y_summed")
        s_oute = sem("y_stored")
        s_done = sem("output_written")

        CREDIT_A, CREDIT_MAC, CREDIT_X2, CREDIT_S3, CREDIT_S3E, CREDIT_R = NA, MACS, 2, 2, 1, 1

        def banks_before(kind, n):
            t, q = divmod(n, BANKS)
            return t * len(kind) + sum(1 for k in kind if k < q)

        def macs_before(n):
            t, q = divmod(n, BANKS)
            return t * MACS + sum(min(FB, F - FB * k) for k in DVE_BANKS if k < q)

        def prologue_then_batches(eng, step, prologue, tail):
            prologue()
            for u in range(2):
                step(0, u, False)
            with eng.Fori(0, NBATCH - 1) as bt:
                for u in range(2, STEPS + 2):
                    step(bt, u, False)
            for u in range(2, STEPS):
                step(NBATCH - 1, u, True)
            tail(NBATCH - 1)

        block = ctx.enter_context(nc.Block())

        @block.sync
        def _(sp):
            sp.dma_start(ids_now[:, :], ids[0:BATCH, :].bitcast(U32)).then_inc(s_ids, 16)
            sp.dma_start(w0_a[:, :, :], w0_pair.rearrange("k r m -> r k m")).then_inc(s_w0, 16)
            sp.dma_start(w0_b[:, :, :], w0_mirror.rearrange("k r m -> r k m")).then_inc(s_w0, 16)
            f1_v = f1.rearrange("(f g) m -> g f m", g=G)
            n = F // W1_CHUNKS
            for c in range(W1_CHUNKS):
                sp.dma_start(w1_raw[:, c * n * G:(c + 1) * n * G].rearrange("p (f m) -> p f m", m=G),
                             f1_v[:, c * n:(c + 1) * n, :]).then_inc(s_w1[c], 16)
            sp.dma_start(w2[:, :, :], f2.rearrange("(f g) m -> g f m", g=G)).then_inc(s_w2, 16)
            with sp.Fori(0, NBATCH - 1) as bt:
                sp.wait_ge(s_gather, (bt + 1) * (16 * F))
                sp.dma_start(ids_now[:, :], ids[bass.ds((bt + 1) * BATCH, BATCH), :].bitcast(U32)) \
                    .then_inc(s_ids, 16)
            for h in range(2):
                sp.wait_ge(s_oute, h + 1)
                sp.dma_start(out.rearrange("b o -> o b")[:, h * 512:(h + 1) * 512],
                             y_row[:, h * 512:(h + 1) * 512]).then_inc(s_done, 16)
            sp.wait_ge(s_done, 32)

        @block.gpsimd
        def _(pool):
            pool.sem_inc(s_x2, CREDIT_X2)

            def gather(f):
                pool.indirect_dma_start(
                    out=x0_rows[:, f, :], out_offset=None, in_=tables[f],
                    in_offset=bass.IndirectOffsetOnAxis(ap=ids_now[:, f:f + 1], axis=0),
                ).then_inc(s_gather, 16)

            def prologue():
                pool.wait_ge(s_ids, 16)
                for f in range(F):
                    gather(f)

            def add_up(bt, u):
                t = terms[:, u % 2]
                pool.wait_ge(s_ya, bt * (STEPS * NA) + NA * (u + 1) + CREDIT_A)
                pool.wait_ge(s_mac, bt * (STEPS * MACS) + MACS * (u + 1) + CREDIT_MAC)
                for i, n in enumerate(TREE):
                    if i:
                        pool.wait_ge(s_tree, bt * (STEPS * len(TREE)) + len(TREE) * u + i)
                    nc.gpsimd.tensor_tensor(t[:, 0:n], t[:, 0:n], t[:, n:2 * n], ALU.add).then_inc(s_tree, 1)
                pool.wait_ge(s_tree, bt * (STEPS * len(TREE)) + len(TREE) * (u + 1))
                pool.wait_ge(s_s3, bt * STEPS + u - 1 + CREDIT_S3)
                nc.gpsimd.tensor_tensor(x2[:, u % 2], t[:, 0], t[:, 1], ALU.add).then_inc(s_x2, 1)

            def step(bt, u, last):
                lo = F - GATHERS_PER_STEP * (GATHER_END - u)
                if not last and 2 < u < GATHER_END:
                    for f in range(lo, lo + GATHERS_PER_STEP):
                        gather(f)
                if not last and u == 2:
                    pool.wait_ge(s_ids, (bt + 2) * 16)
                    pool.wait_ge(s_parts, (bt + 1) * 2)
                add_up(bt, u)
                if not last and u == 2:
                    for f in range(lo + GATHERS_PER_STEP):
                        gather(f)

            prologue_then_batches(pool, step, prologue, lambda bt: None)

        @block.tensor
        def _(pe):
            pe.sem_inc(s_s3, CREDIT_S3)

            def turn(bt, r, s3_stored=None):
                pe.wait_ge(s_parts, (bt + 1) * 2)
                if r % 2:
                    pe.wait_ge(s_cols, bt * 4 + r)
                elif s3_stored is not None:
                    pe.wait_ge(s_s3e, s3_stored + CREDIT_S3E)
                elif r:
                    pe.wait_ge(s_cols, bt * 4 + r)
                for i in range(4):
                    mm = nc.tensor.transpose(ps[0:HL, MISC_BANK, i * P:(i + 1) * P],
                                             x0_parts[:, 4 * r + i, :].bitcast(F32), eye[:, :])
                mm.then_inc(s_turn, 1)

            def pick(gf, j, k):
                if k == 0 and j % GROUPS == 0:
                    pe.wait_ge(s_cols, gf + 4)
                if k == 2:
                    pe.wait_ge(s_copy, gf + 1)
                elif k > 2:
                    pe.wait_ge(s_pair, gf * KT + k - 2)
                elif j > 0:
                    pe.wait_ge(s_pair, gf * KT + k - 1)
                nc.tensor.matmul(ps[0:KR, SEL_BANKS[k % 2], :], sel[:, k, :],
                                 x0_cols[:, j % GROUPS * GCOLS:(j % GROUPS + 1) * GCOLS],
                                 start=True, stop=True).then_inc(s_pick, 1)

            def turn_scalars(gf, j, s3_stored=None):
                pe.wait_ge(s_scal, gf)
                if s3_stored is not None:
                    pe.wait_ge(s_s3e, s3_stored + CREDIT_S3E)
                for t in range(TILES):
                    at = (j % GROUPS * TILES + t) * P
                    mm = nc.tensor.matmul(ps[:, MISC_BANK, t * FX:(t + 1) * FX], x0_cols[:, at:at + P],
                                          both[:, :], start=True, stop=True)
                mm.then_inc(s_st, 1)

            def cin1(gf, k):
                if k == 0:
                    pe.wait_ge(s_r1, gf)
                pe.wait_ge(s_pair, gf * KT + k + 1)
                mm = nc.tensor.matmul(ps[:, X1_BANK, :], w0_a[:, k, :], pairs[:, k, :],
                                      start=(k == 0), stop=(k == KT - 1))
                if k == KT - 1:
                    mm.then_inc(s_x1, 1)

            def cin2(bt, u, q):
                n = BANKS * u + q
                old = n - RING
                if old % BANKS in ACT_BANKS:
                    pe.wait_ge(s_ya, bt * (STEPS * NA) + banks_before(ACT_BANKS, old + 1) + CREDIT_A)
                else:
                    pe.wait_ge(s_mac, bt * (STEPS * MACS) + macs_before(old + 1) + CREDIT_MAC)
                if u % TILES == 0 and q == 0:
                    pe.wait_ge(s_x1h, bt * GROUPS + u // TILES + 1)
                    pe.wait_ge(s_x1l, bt * GROUPS + u // TILES + 1)
                par, at = u // TILES % 2, u % TILES * P
                width = min(FB, F - FB * q) * G
                y = ps[:, n % RING, 0:width]
                high = w1_high[:, q * FB * G:q * FB * G + width]
                low = w1_low[:, q * FB * G:q * FB * G + width]
                nc.tensor.matmul(y, x1_high[:, par, at:at + P], high, start=True, stop=False)
                nc.tensor.matmul(y, x1_high[:, par, at:at + P], low, start=False, stop=False)
                nc.tensor.matmul(y, x1_low[:, par, at:at + P], high, start=False, stop=True) \
                    .then_inc(s_y, 1)

            def sum_s3(bt, u, scalars=NGROUP, cols=4 * NBATCH):
                pe.wait_ge(s_x2, bt * STEPS + u - 1 + CREDIT_X2)
                pe.wait_ge(s_diag, bt * STEPS + u - 1)
                pe.wait_ge(s_s3e, bt * STEPS + u - 2 + CREDIT_S3E)
                if u == 2:
                    pe.wait_ge(s_r, bt * 2 + CREDIT_R)
                if u % TILES == 1:
                    pe.wait_ge(s_scal, scalars)
                if u == GATHER_END:
                    pe.wait_ge(s_cols, cols)
                nc.tensor.matmul(ps[:, MISC_BANK, 0:TB * FX], x2[:, u % 2, :],
                                 x0_diag[:, u % 2].rearrange("p b f -> p (b f)"),
                                 start=True, stop=True).then_inc(s_s3, 1)

            def cin3(bt, lo, hi):
                if lo == 0:
                    pe.wait_ge(s_s3e, bt * STEPS + STEPS + CREDIT_S3E)
                for f in range(lo, hi):
                    mm = nc.tensor.matmul(ps[:, MISC_BANK, 0:BATCH], w2[:, f, :], s3[:, f, :],
                                          start=(f == 0), stop=(f == F - 1))
                if hi == F:
                    mm.then_inc(s_l3, 1)

            def prologue():
                pe.wait_ge(s_const, 16 * 4)
                pe.wait_ge(s_sel, 2)
                pe.wait_ge(s_top, 16 * 7)
                for c in range(NBATCH // 4):
                    for i in range(4):
                        mm = nc.tensor.transpose(ps[0:DENSE, c, i * P:(i + 1) * P],
                                                 dense_rows[:, 4 * c + i, :], eye[:, :])
                    mm.then_inc(s_den, 1)
                for r in range(4):
                    turn(0, r)
                pick(0, 0, 0)
                turn_scalars(0, 0)
                for k in range(KT):
                    pick(0, 0, k + 1)
                pe.wait_ge(s_w0s, 1)
                for k in range(KT):
                    cin1(0, k)
                pe.wait_ge(s_w1h, W1_CHUNKS)
                pe.wait_ge(s_w1l, W1_CHUNKS)
                pe.wait_ge(s_dene, NBATCH // 4)
                pe.wait_ge(s_w2, 16)

            def step(bt, u, last):
                tile, j = u % TILES, u // TILES + 1
                front = not (last and j == GROUPS)
                gf = bt * GROUPS + j
                for q in range(BANKS):
                    cin2(bt, u, q)
                    if q == 4 and u >= 2:
                        sum_s3(bt, u, gf + 1 if front else NGROUP, bt * 4 + 6 if front else 4 * NBATCH)
                    if front and j == GROUPS and (tile, q) in TURNS:
                        turn(bt + 1, TURNS.index((tile, q)), bt * STEPS + (u - 2 if q < 4 else u - 1))
                    if front and (tile, q) == SCALARS:
                        turn_scalars(gf, j, bt * STEPS + u - 2 if u > 2 else None)
                    if front and (tile, q) in PICKS:
                        pick(gf, j, PICKS.index((tile, q)))
                    if front and (tile, q) in CIN1:
                        cin1(gf, CIN1.index((tile, q)))
                    if u == STEPS + 1 and q >= 6:
                        cin3(bt, (q - 6) * 10, min((q - 5) * 10, F))

            def tail(bt):
                sum_s3(bt, STEPS)
                sum_s3(bt, STEPS + 1)
                cin3(bt, 0, F)
                pe.wait_ge(s_r, 2 * NBATCH + CREDIT_R)
                pe.wait_ge(s_r1, NGROUP)
                for h in range(2):
                    cols = slice(h * 512, (h + 1) * 512)
                    for c in range(H1 // P):
                        for k, x in enumerate((r1, r2, r3)):
                            nc.tensor.matmul(ps[:, 4 * h + c, :], wt1[:, k, c * P:(c + 1) * P], x[:, cols],
                                             start=(k == 0), stop=False)
                        nc.tensor.matmul(ps[:, 4 * h + c, :], wt1_dense[:, c * P:(c + 1) * P],
                                         dense_t[:, cols], start=False, stop=True).then_inc(s_h1, 1)
                for h in range(2):
                    pe.wait_ge(s_h1e, 4 * h + 4)
                    for c in range(H2 // P):
                        for k in range(H1 // P):
                            mm = nc.tensor.matmul(ps[:, 2 * h + c, :], wt2[:, k, c * P:(c + 1) * P],
                                                  h1[:, h, k, :], start=(k == 0), stop=(k == H1 // P - 1))
                        mm.then_inc(s_h2, 1)
                for h in range(2):
                    pe.wait_ge(s_h2e, 2 * h + 2)
                    for k in range(H2 // P):
                        mm = nc.tensor.matmul(ps[0:1, 4 + h, :], wt3[:, k:k + 1], h2[h][:, k, :],
                                              start=(k == 0), stop=(k == H2 // P - 1))
                    mm.then_inc(s_out, 1)

            prologue_then_batches(pe, step, prologue, tail)

        @block.scalar
        def _(act):
            act.dma_start(eye[:, :], c_eye[:, :]).then_inc(s_const, 16)
            act.dma_start(sel_raw[:, :], c_sel[:, :]).then_inc(s_const, 16)
            act.dma_start(both_raw[:, :], c_both[:, :]).then_inc(s_const, 16)
            act.dma_start(mask[:, :], c_mask[:, :]).then_inc(s_const, 16)
            act.dma_start(wt1[:, :, :], w_top1[0:3 * P, :].rearrange("(k p) n -> p k n", p=P)) \
                .then_inc(s_top, 16)
            act.dma_start(wt1_dense[:, :], w_top1[3 * P:3 * P + DENSE, :]).then_inc(s_top, 16)
            act.dma_start(wt2[:, :, :], w_top2.rearrange("(k p) n -> p k n", p=P)).then_inc(s_top, 16)
            act.dma_start(wt3[:, :], w_top3[:, :]).then_inc(s_top, 16)
            act.dma_start(bt1[:, :], b_top1[:, :]).then_inc(s_top, 16)
            act.dma_start(bt2[:, :], b_top2[:, :]).then_inc(s_top, 16)
            act.dma_start(dense_rows[:, :, :], dense_ctx.rearrange("(c p) k -> p c k", p=P)) \
                .then_inc(s_top, 16)
            act.sem_inc(s_ya, CREDIT_A)
            act.sem_inc(s_s3e, CREDIT_S3E)
            act.sem_inc(s_r, CREDIT_R)

            def store_cols(bt, r):
                act.wait_ge(s_turn, bt * 4 + r + 1)
                nc.scalar.activation(
                    x0_cols[:, :].rearrange("k (b d) -> k d b", d=D)[:, 4 * r:4 * r + 4, :],
                    ps[0:HL, MISC_BANK, :].rearrange("k (d b) -> k d b", d=4), ACT.Copy).then_inc(s_cols, 1)

            def store_copy(gf):
                act.wait_ge(s_pick, gf * (1 + KT) + 1)
                nc.scalar.activation(x0_copy[:, :], ps[0:KR, SEL_BANKS[0], :], ACT.Copy).then_inc(s_copy, 1)

            def store_scalars(gf, j, guard):
                act.wait_ge(s_st, gf + 1)
                if guard:
                    act.wait_ge(s_diag, (gf - 1) * TILES)
                nc.scalar.activation(x0_scal[:, j % 2].rearrange("p t f -> p (t f)"),
                                     ps[:, MISC_BANK, 0:TILES * FX], ACT.Copy).then_inc(s_scal, 1)

            def store_x1(gf, j):
                act.wait_ge(s_x1, gf + 1)
                nc.scalar.activation(x1_high[:, j % 2, :], ps[:, X1_BANK, :], ACT.Copy).then_inc(s_x1h, 1)

            def scale(bt, u, q):
                if q == ACT_BANKS[0]:
                    act.wait_ge(s_x2, bt * STEPS + u - 1 + CREDIT_X2)
                    if u % TILES == 0:
                        act.wait_ge(s_scal, bt * GROUPS + u // TILES + 1)
                act.wait_ge(s_y, bt * (STEPS * BANKS) + BANKS * u + q + 1)
                for i in range(FB):
                    f = FB * q + i
                    op = nc.scalar.activation(
                        terms[:, u % 2, FB * ACT_BANKS.index(q) + i, :],
                        ps[:, (BANKS * u + q) % RING, i * G:(i + 1) * G], ACT.Copy,
                        scale=x0_scal[:, u // TILES % 2, u % TILES, f:f + 1])
                op.then_inc(s_ya, 1)

            def store_s3(bt, u):
                if u == 2:
                    act.wait_ge(s_r, bt * 2 + CREDIT_R)
                act.wait_ge(s_s3, bt * STEPS + u - 1 + CREDIT_S3)
                at = (u - 2) * TB
                nc.scalar.activation(s3[:, :, at:at + TB],
                                     ps[:, MISC_BANK, 0:TB * FX].rearrange("p (b f) -> p f b", f=FX),
                                     ACT.Copy).then_inc(s_s3e, 1)

            def store_r(bt):
                act.wait_ge(s_s3e, bt * STEPS + STEPS + CREDIT_S3E)
                nc.scalar.activation(r2[:, bass.ds(bt * BATCH, BATCH)], s3[:, F, :], ACT.Copy).then_inc(s_r, 1)
                act.wait_ge(s_l3, bt + 1)
                nc.scalar.activation(r3[:, bass.ds(bt * BATCH, BATCH)], ps[:, MISC_BANK, 0:BATCH],
                                     ACT.Copy).then_inc(s_r, 1)

            def prologue():
                n = F // W1_CHUNKS * G
                for c in range(W1_CHUNKS):
                    act.wait_ge(s_w1[c], 16)
                    nc.scalar.activation(w1_high[:, c * n:(c + 1) * n], w1_raw[:, c * n:(c + 1) * n],
                                         ACT.Copy).then_inc(s_w1h, 1)
                for c in range(NBATCH // 4):
                    act.wait_ge(s_den, c + 1)
                    nc.scalar.activation(dense_t[:, c * 512:(c + 1) * 512], ps[0:DENSE, c, :],
                                         ACT.Copy).then_inc(s_dene, 1)
                for r in range(4):
                    store_cols(0, r)
                store_copy(0)
                store_scalars(0, 0, False)
                store_x1(0, 0)

            def step(bt, u, last):
                tile, j = u % TILES, u // TILES + 1
                front = not (last and j == GROUPS)
                gf = bt * GROUPS + j
                for q in range(BANKS):
                    if q in ACT_BANKS:
                        scale(bt, u, q)
                    if q == 5 and u >= 2:
                        store_s3(bt, u)
                    if front and j == GROUPS and (tile, q) in TURNS:
                        store_cols(bt + 1, TURNS.index((tile, q)))
                    if front and (tile, q) == PICKS[0]:
                        store_copy(gf)
                    if front and (tile, q) == SCALARS:
                        store_scalars(gf, j, True)
                    if front and (tile, q) == STORE_X1:
                        store_x1(gf, j)
                if u == STEPS + 1:
                    store_r(bt)

            def tail(bt):
                store_s3(bt, STEPS)
                store_s3(bt, STEPS + 1)
                store_r(bt)
                for h in range(2):
                    for c in range(H1 // P):
                        act.wait_ge(s_h1, 4 * h + c + 1)
                        nc.scalar.activation(h1[:, h, c, :], ps[:, 4 * h + c, :], ACT.Relu,
                                             bias=bt1[:, c:c + 1]).then_inc(s_h1e, 1)
                for h in range(2):
                    for c in range(H2 // P):
                        act.wait_ge(s_h2, 2 * h + c + 1)
                        nc.scalar.activation(h2[h][:, c, :], ps[:, 2 * h + c, :], ACT.Relu,
                                             bias=bt2[:, c:c + 1]).then_inc(s_h2e, 1)
                for h in range(2):
                    act.wait_ge(s_out, h + 1)
                    nc.scalar.activation(y_row[:, h * 512:(h + 1) * 512], ps[0:1, 4 + h, :],
                                         ACT.Copy).then_inc(s_oute, 1)

            prologue_then_batches(act, step, prologue, tail)

        @block.vector
        def _(dve):
            dve.sem_inc(s_mac, CREDIT_MAC)

            def split_x0(bt):
                dve.wait_ge(s_gather, (bt + 1) * (16 * F))
                dve.wait_ge(s_turn, bt * 4)
                rows = x0_rows[:, :, :].rearrange("p f d -> p d f")
                nc.vector.tensor_copy(x0_parts[:, :, 0:F], rows).then_inc(s_parts, 1)
                dve.wait_ge(s_parts, bt * 2 + 1)
                nc.vector.tensor_tensor(x0_parts[:, :, LOW:LOW + F], rows, x0_parts[:, :, 0:F].bitcast(F32),
                                        ALU.subtract).then_inc(s_parts, 1)

            def multiply(gf, k):
                dve.wait_ge(s_pick, gf * (1 + KT) + k + 2)
                if k == 0:
                    dve.wait_ge(s_copy, gf + 1)
                    dve.wait_ge(s_x1, gf)
                nc.vector.tensor_tensor(pairs[:, k, :], ps[0:KR, SEL_BANKS[(k + 1) % 2], :], x0_copy[:, :],
                                        ALU.mult).then_inc(s_pair, 1)

            def split_x1(gf, j):
                dve.wait_ge(s_x1h, gf + 1)
                nc.vector.tensor_tensor(x1_low[:, j % 2, :], ps[:, X1_BANK, :],
                                        x1_high[:, j % 2, :].bitcast(F32), ALU.subtract).then_inc(s_x1l, 1)
                nc.vector.tensor_reduce(r1[:, bass.ds(gf * (GCOLS // D), GCOLS // D)],
                                        ps[:, X1_BANK, :].rearrange("p (b d) -> p b d", d=D),
                                        AX_X, ALU.add).then_inc(s_r1, 1)

            def mac(bt, u, q):
                if q == DVE_BANKS[0]:
                    dve.wait_ge(s_ya, bt * (STEPS * NA) + NA * u + 1 + CREDIT_A)
                    if u % TILES == 0:
                        dve.wait_ge(s_scal, bt * GROUPS + u // TILES + 1)
                dve.wait_ge(s_y, bt * (STEPS * BANKS) + BANKS * u + q + 1)
                done = macs_before(q)
                for i in range(min(FB, F - FB * q)):
                    f, n = FB * q + i, done + i
                    acc = terms[:, u % 2, n % CHAINS, :]
                    y = ps[:, (BANKS * u + q) % RING, i * G:(i + 1) * G]
                    x0 = x0_scal[:, u // TILES % 2, u % TILES, f:f + 1]
                    if n >= CHAINS:
                        dve.wait_ge(s_mac, bt * (STEPS * MACS) + MACS * u + n - CHAINS + 1 + CREDIT_MAC)
                    nc.vector.scalar_tensor_tensor(out=acc, in0=y, scalar=x0, in1=acc, op0=ALU.mult,
                                                   op1=ALU.add).then_inc(s_mac, 1)

            def diagonal(bt, u):
                dve.wait_ge(s_s3, bt * STEPS + u - 2 + CREDIT_S3)
                t = u - 1
                nc.vector.tensor_tensor(
                    x0_diag[:, t % 2],
                    x0_scal[:, t // TILES % 2, t % TILES, :].unsqueeze(1).to_broadcast([P, TB, FX]),
                    mask[:, :].unsqueeze(2).to_broadcast([P, TB, FX]), ALU.mult).then_inc(s_diag, 1)

            def prologue():
                nc.vector.memset(x0_parts[:, :, :].bitcast(F32), 0.0).then_inc(s_clear, 1)
                dve.wait_ge(s_clear, 1)
                nc.vector.memset(x0_parts[:, :, F:FX].bitcast(F32), 1.0).then_inc(s_clear, 1)
                dve.wait_ge(s_const, 16 * 4)
                nc.vector.tensor_copy(sel[:, :, :].rearrange("k a b -> k (a b)"), sel_raw[:, :]) \
                    .then_inc(s_sel, 1)
                nc.vector.tensor_copy(both[:, :], both_raw[:, :]).then_inc(s_sel, 1)
                dve.wait_ge(s_w0, 32)
                nc.vector.tensor_tensor(w0_a[:, :, :], w0_a[:, :, :], w0_b[:, :, :], ALU.add) \
                    .then_inc(s_w0s, 1)
                n = F // W1_CHUNKS * G
                for c in range(W1_CHUNKS):
                    dve.wait_ge(s_w1h, c + 1)
                    nc.vector.tensor_tensor(w1_low[:, c * n:(c + 1) * n], w1_raw[:, c * n:(c + 1) * n],
                                            w1_high[:, c * n:(c + 1) * n].bitcast(F32), ALU.subtract) \
                        .then_inc(s_w1l, 1)
                dve.wait_ge(s_clear, 2)
                split_x0(0)
                for k in range(KT):
                    multiply(0, k)
                split_x1(0, 0)

            def step(bt, u, last):
                tile, j = u % TILES, u // TILES + 1
                front = not (last and j == GROUPS)
                gf = bt * GROUPS + j
                for q in range(BANKS):
                    if q in DVE_BANKS:
                        mac(bt, u, q)
                    if q == 2 and u >= 1:
                        diagonal(bt, u)
                    if front and (tile, q) in PICKS[1:]:
                        multiply(gf, PICKS.index((tile, q)) - 1)
                    if front and (tile, q) == SPLIT_X1:
                        split_x1(gf, j)
                    if not last and (u, q) == (GATHER_END - 1, BANKS - 1):
                        split_x0(bt + 1)

            prologue_then_batches(dve, step, prologue, lambda bt: diagonal(bt, STEPS))


TOP = ("W_top1", "b_top1", "W_top2", "b_top2", "W_top3")


def kernel(**inputs):
    import concourse.bacc as bacc
    from concourse.bass_utils import run_bass_kernel_spmd

    rows, mirror = pair_rows()
    f0 = np.asarray(inputs["L0_rec_f0"])
    w0_pair = np.zeros((KT * KR, G), f0.dtype)
    w0_pair[:SHIFTS * F] = f0[rows]
    w0_mirror = np.zeros((KT * KR, G), f0.dtype)
    w0_mirror[F:SHIFTS * F] = f0[mirror]
    c_sel, c_both, c_mask, c_eye = selectors()
    named = {"dense_ctx": inputs["dense_ctx"], "ids": inputs["ids"]}
    named |= {f"tbl_{f}": inputs[f"tbl_{f}"] for f in range(F)}
    named |= {name: inputs[name] for name in TOP}
    for name in ("b_top1", "b_top2", "W_top3"):
        named[name] = np.asarray(inputs[name]).reshape(-1, P).T
    named |= {"w0_pair": w0_pair.reshape(KT, KR, G), "w0_mirror": w0_mirror.reshape(KT, KR, G),
              "f1": inputs["L0_rec_f1"], "f2": inputs["L0_rec_f2"],
              "c_sel": c_sel, "c_both": c_both, "c_mask": c_mask, "c_eye": c_eye}
    nc = bacc.Bacc("TRN2", target_bir_lowering=False, num_devices=1)
    arrays, ap = {}, {}
    for name, x in named.items():
        a = np.ascontiguousarray(x)
        arrays["in_" + name] = a
        ap[name] = nc.dram_tensor("in_" + name, a.shape, mybir.dt.from_np(a.dtype), kind="ExternalInput").ap()
    out = nc.dram_tensor("out_y", (B, 1), F32, kind="ExternalOutput").ap()
    cin_tower(nc, ap["dense_ctx"], ap["ids"], [ap[f"tbl_{f}"] for f in range(F)],
              *[ap[name] for name in TOP], ap["w0_pair"], ap["w0_mirror"], ap["f1"], ap["f2"],
              ap["c_sel"], ap["c_both"], ap["c_mask"], ap["c_eye"], out)
    r = run_bass_kernel_spmd(nc, [arrays], core_ids=[0])
    return r.results[0]["out_y"]
```

```python
from contextlib import ExitStack

import numpy as np

import concourse.bass as bass
from concourse import mybir

F32 = mybir.dt.float32
F32R = mybir.dt.float32r
U32 = mybir.dt.uint32
ALU = mybir.AluOpType
ACT = mybir.ActivationFunctionType
AX_X = mybir.AxisListType.X

P = 128
B, F, D, G = 1024, 39, 16, 128
H1, H2 = 512, 256
DENSE = 16
TB = P // D
TILES = 4
GCOLS = TILES * P
BATCH = P
GROUPS = BATCH * D // GCOLS
STEPS = GROUPS * TILES
NBATCH = B // BATCH
NGROUP = GROUPS * NBATCH

SHIFTS = F // 2 + 1
SPT = P // F
KT = -(-SHIFTS // SPT)
KR = SPT * F
FX = F + 1
CYCLIC = KR + KT - 1

FB = 4
BANKS = -(-F // FB)
RING = 5
ACT_BANKS = (0, 3, 5, 7)
NA = len(ACT_BANKS)
DVE_BANKS = tuple(q for q in range(BANKS) if q not in ACT_BANKS)
MACS = sum(min(FB, F - FB * q) for q in DVE_BANKS)
CHAINS = 2
TERMS = NA * FB
W1_CHUNKS = 3
S3_BANK, X1_BANK, MISC_BANK = 5, 6, 7
SPLIT = (0, 1, 2, 3, 4)
NS = len(SPLIT)
CIN1_ORDER = (0, 1, 5, 6, 4, 2, 3)
PRODUCTS = ((0, 1), (0, 4), (0, 7), (0, 9), (1, 4), (1, 7), (2, 1))
SCALARS = (1, 0)
S3_AT = 5
HIGHS = ((0, 4), (0, 7), (1, 0), (1, 4), (1, 7))
POOL_LOWS = {0: (0, 1), 1: (3,)}
DVE_LOWS = {2: (1, 3), 4: (2, 0)}
CIN1 = ((1, 6), (1, 9), (2, 2), (2, 5), (2, 8), (3, 1), (3, 4))
STORE_X1, SPLIT_X1 = (3, 4), (3, 5)
CIN3 = (7, 8, 9)
L1_BANKS = ((6, 0, 1, 2), (3, 4, 0, 1))
L2_BANKS = ((6, 2), (3, 4))
L3_BANKS = (5, 2)
ROWS_AT = (9, 3)
TURNS = ((9, 7), (10, 0), (10, 4), (10, 8))
TREE = (8, 4, 2)


def layout_constants():
    mask = (np.arange(P)[:, None] // D == np.arange(TB)[None, :]).astype(np.float32)
    return mask, np.eye(P, dtype=np.float32)


def pair_rows():
    k, i, f = np.ogrid[:KT, :SPT, :F]
    g, h = (f - KT * i) % F, (f + k) % F
    apart = KT * i + k + 0 * f
    return g * F + h, h * F + g, apart


def cin_tower(nc, dense_ctx, ids, tables, w_top1, b_top1, w_top2, b_top2, w_top3,
              w0_pair, w0_mirror, f1, f2, c_mask, c_eye, out):
    with ExitStack() as ctx:
        def sb(name, shape, dt=F32):
            return ctx.enter_context(nc.sbuf_tensor(name, shape, dt))

        def sem(name):
            return ctx.enter_context(nc.semaphore(name))

        w1_high = sb("w1_high", [P, F * G], F32R)
        w1_low = sb("w1_low", [P, F * G], F32R)
        w2 = sb("w2", [P, F, G])
        w0 = sb("w0", [KR, KT, G])
        w0_high = sb("w0_high", [KR, NS, G], F32R)
        w0_low = sb("w0_low", [KR, NS, G], F32R)
        mask = sb("mask", [P, TB])
        eye = sb("eye", [P, P])
        ids_now = sb("ids_now", [P, F], U32)
        x0_in = sb("x0_in", [P, F, D])
        x0_rows = sb("x0_rows", [P, CYCLIC * D])
        x0_cols = sb("x0_cols", [CYCLIC, BATCH * D])
        x0_first = sb("x0_first", [KR, 2, GCOLS])
        prods = sb("prods", [P, KT, GCOLS])
        prods_high = sb("prods_high", [KR, NS, GCOLS], F32R)
        prods_low = sb("prods_low", [KR, NS, GCOLS], F32R)
        x1_high = sb("x1_high", [P, 2, GCOLS], F32R)
        x1_low = sb("x1_low", [P, 2, GCOLS], F32R)
        x0_scal = sb("x0_scal", [P, 2, TILES, FX])
        x0_diag = sb("x0_diag", [P, 2, TB, FX])
        terms = sb("terms", [P, 2, TERMS, G])
        x2 = sb("x2", [P, 2, G])
        s3 = sb("s3", [P, FX, BATCH])
        r1 = sb("r1", [P, B])
        r2 = sb("r2", [P, B])
        r3 = sb("r3", [P, B])
        wt1 = sb("wt1", [P, 3, H1])
        wt1_dense = sb("wt1_dense", [DENSE, H1])
        wt2 = sb("wt2", [P, H1 // P, H2])
        wt3 = sb("wt3", [P, H2 // P])
        bt1 = sb("bt1", [P, H1 // P])
        bt2 = sb("bt2", [P, H2 // P])
        dense_rows = sb("dense_rows", [P, NBATCH, DENSE])
        dense_t = sb("dense_t", [DENSE, B])
        w1_raw = s3[:, :, :].rearrange("p f b -> p (f b)")[:, 0:F * G]
        terms_flat = terms[:, :, :, :].rearrange("p a t g -> p (a t g)")
        w0_a, w0_b = (terms_flat[0:KR, i * KT * G:(i + 1) * KT * G] for i in range(2))
        h1 = terms_flat[:, 0:2 * H1 // P * 512].rearrange("p (h c n) -> p h c n", h=2, c=H1 // P)
        h2 = prods[:, 0:2 * H2 // P, :].rearrange("p (h c) n -> p h c n", h=2)
        y_row = x0_cols[0:1, 0:B]

        ps = ctx.enter_context(nc.psum_tensor("ps", [P, 8, 512], F32))

        s_ids = sem("ids_loaded")
        s_const = sem("constants_loaded")
        s_w1 = [sem(f"w1_loaded{c}") for c in range(W1_CHUNKS)]
        s_w0 = sem("w0_loaded")
        s_w2 = sem("w2_loaded")
        s_top = sem("mlp_weights_loaded")
        s_gather = sem("rows_gathered")
        s_ones = sem("ones_set")
        s_w1h = sem("w1_high_ready")
        s_w1l = sem("w1_low_ready")
        s_w0s = sem("w0_folded")
        s_w0h = sem("w0_high_ready")
        s_w0l = sem("w0_low_ready")
        s_rows = sem("rows_put_aside")
        s_turn = sem("x0_transposed")
        s_cols = sem("x0_cols_stored")
        s_first = [sem(f"first_factor_moved{i}") for i in range(2)]
        s_second = [sem(f"second_factor_moved{k}") for k in range(1, KT)]
        s_prod = sem("products_ready")
        s_high = sem("product_highs_ready")
        s_plow = sem("product_lows_by_pool")
        s_vlow = sem("product_lows_by_vector")
        s_x1 = sem("x1_summed")
        s_x1h = sem("x1_high_ready")
        s_x1l = sem("x1_low_ready")
        s_r1 = sem("r1_ready")
        s_st = sem("scalars_turned")
        s_scal = sem("scalars_stored")
        s_y = sem("y_bank_ready")
        s_ya = sem("y_bank_scaled")
        s_mac = sem("macs_done")
        s_tree = sem("partial_adds")
        s_x2 = sem("x2_ready")
        s_diag = sem("x0_diag_ready")
        s_s3 = sem("s3_summed")
        s_s3e = sem("s3_stored")
        s_l3 = sem("r3_summed")
        s_r = sem("r2_r3_stored")
        s_den = sem("dense_turned")
        s_dene = sem("dense_stored")
        s_h1 = sem("h1_summed")
        s_h1e = sem("h1_stored")
        s_h2 = sem("h2_summed")
        s_h2e = sem("h2_stored")
        s_out = sem("y_summed")
        s_oute = sem("y_stored")
        s_done = sem("output_written")

        CREDIT_A, CREDIT_MAC, CREDIT_X2, CREDIT_S3, CREDIT_S3E, CREDIT_R = NA, MACS, 2, 2, 1, 1

        POOL_PARTS = [i for parts in POOL_LOWS.values() for i in parts]

        def low_ready(gf, i):
            if i in DVE_LOWS:
                return s_vlow, (gf - 1) * len(DVE_LOWS) + list(DVE_LOWS).index(i) + 1
            return s_plow, (gf - 1) * len(POOL_PARTS) + POOL_PARTS.index(i) + 1

        def split_low(eng, gf, i):
            eng.wait_ge(s_high, (gf - 1) * NS + i + 1)
            eng.tensor_tensor(prods_low[:, i, :], prods[0:KR, SPLIT[i], :],
                              prods_high[:, i, :].bitcast(F32), ALU.subtract).then_inc(low_ready(gf, i)[0], 1)

        def banks_before(kind, n):
            t, q = divmod(n, BANKS)
            return t * len(kind) + sum(1 for k in kind if k < q)

        def macs_before(n):
            t, q = divmod(n, BANKS)
            return t * MACS + sum(min(FB, F - FB * k) for k in DVE_BANKS if k < q)

        def prologue_then_batches(eng, step, prologue, tail):
            prologue()
            for u in range(2):
                step(0, u, False)
            with eng.Fori(0, NBATCH - 1) as bt:
                for u in range(2, STEPS + 2):
                    step(bt, u, False)
            for u in range(2, STEPS):
                step(NBATCH - 1, u, True)
            tail(NBATCH - 1)

        block = ctx.enter_context(nc.Block())

        @block.sync
        def _(sp):
            sp.dma_start(ids_now[:, :], ids[0:BATCH, :].bitcast(U32)).then_inc(s_ids, 16)
            sp.dma_start(w0_a.rearrange("r (k m) -> r k m", m=G), w0_pair.rearrange("k r m -> r k m")) \
                .then_inc(s_w0, 16)
            sp.dma_start(w0_b.rearrange("r (k m) -> r k m", m=G), w0_mirror.rearrange("k r m -> r k m")) \
                .then_inc(s_w0, 16)
            f1_v = f1.rearrange("(f g) m -> g f m", g=G)
            n = F // W1_CHUNKS
            for c in range(W1_CHUNKS):
                sp.dma_start(w1_raw[:, c * n * G:(c + 1) * n * G].rearrange("p (f m) -> p f m", m=G),
                             f1_v[:, c * n:(c + 1) * n, :]).then_inc(s_w1[c], 16)
            sp.dma_start(w2[:, :, :], f2.rearrange("(f g) m -> g f m", g=G)).then_inc(s_w2, 16)

            def load_ids(bt):
                sp.wait_ge(s_gather, bt * (16 * F))
                sp.dma_start(ids_now[:, :], ids[bass.ds(bt * BATCH, BATCH), :].bitcast(U32)) \
                    .then_inc(s_ids, 16)

            def move_first(j):
                at = j % GROUPS * GCOLS
                for i in range(SPT):
                    row = -KT * i % F
                    sp.dma_start(x0_first[i * F:(i + 1) * F, j % 2, :], x0_cols[row:row + F, at:at + GCOLS]) \
                        .then_inc(s_first[j % 2], 16)

            def move(gf, j):
                if j > 0:
                    sp.wait_ge(s_x1, gf)
                if j % GROUPS == 0:
                    move_first(j)
                at = j % GROUPS * GCOLS
                for k in range(1, KT):
                    sp.dma_start(prods[0:KR, k, :], x0_cols[k:k + KR, at:at + GCOLS]).then_inc(s_second[k - 1], 16)
                if j == 0:
                    sp.wait_ge(s_cols, 4)
                if j % GROUPS < GROUPS - 1:
                    move_first(j + 1)

            load_ids(1)
            sp.wait_ge(s_cols, 1)
            move(0, 0)
            with sp.Fori(0, NBATCH - 2) as bt:
                for j in range(1, GROUPS):
                    move(bt * GROUPS + j, j)
                load_ids(bt + 2)
                move(bt * GROUPS + GROUPS, GROUPS)
            for gf in range((NBATCH - 2) * GROUPS + 1, NGROUP):
                move(gf, gf % GROUPS or GROUPS)
            for h in range(2):
                sp.wait_ge(s_oute, h + 1)
                sp.dma_start(out.rearrange("b o -> o b")[:, h * 512:(h + 1) * 512],
                             y_row[:, h * 512:(h + 1) * 512]).then_inc(s_done, 16)
            sp.wait_ge(s_done, 32)

        @block.gpsimd
        def _(pool):
            pool.sem_inc(s_x2, CREDIT_X2)

            def gather(f):
                pool.indirect_dma_start(
                    out=x0_in[:, f, :], out_offset=None, in_=tables[f],
                    in_offset=bass.IndirectOffsetOnAxis(ap=ids_now[:, f:f + 1], axis=0),
                ).then_inc(s_gather, 16)

            def prologue():
                pool.wait_ge(s_ids, 16)
                for f in range(F):
                    gather(f)

            def add_up(bt, u, front=True):
                gf = bt * GROUPS + u // TILES + 1
                if front:
                    for i in POOL_LOWS.get(u % TILES, ()):
                        split_low(pool, gf, i)
                t = terms[:, u % 2]
                pool.wait_ge(s_ya, bt * (STEPS * NA) + NA * (u + 1) + CREDIT_A)
                pool.wait_ge(s_mac, bt * (STEPS * MACS) + MACS * (u + 1) + CREDIT_MAC)
                for i, n in enumerate(TREE):
                    if i:
                        pool.wait_ge(s_tree, bt * (STEPS * len(TREE)) + len(TREE) * u + i)
                    nc.gpsimd.tensor_tensor(t[:, 0:n], t[:, 0:n], t[:, n:2 * n], ALU.add).then_inc(s_tree, 1)
                pool.wait_ge(s_tree, bt * (STEPS * len(TREE)) + len(TREE) * (u + 1))
                pool.wait_ge(s_s3, bt * STEPS + u - 1 + CREDIT_S3)
                nc.gpsimd.tensor_tensor(x2[:, u % 2], t[:, 0], t[:, 1], ALU.add).then_inc(s_x2, 1)

            def share(done, n, steps):
                left = F - done
                return range(done + left * n // steps, done + left * (n + 1) // steps)

            prologue()
            pool.wait_ge(s_ids, 2 * 16)
            pool.wait_ge(s_rows, 3)
            wanted, ahead = ROWS_AT[0], 12
            for f in range(ahead):
                gather(f)
            for u in range(wanted):
                if u < wanted - 1:
                    for f in share(ahead, u, wanted - 1):
                        gather(f)
                add_up(0, u)
            with pool.Fori(0, NBATCH - 2) as bt:
                pool.wait_ge(s_ids, (bt + 3) * 16)
                pool.wait_ge(s_rows, bt * 2 + 5)
                add_up(bt, wanted)
                for n in range(STEPS - 1):
                    for f in share(0, n, STEPS - 1):
                        gather(f)
                    add_up(bt, wanted + 1 + n)
            for u in range(wanted, 2 * STEPS):
                add_up(NBATCH - 2, u, u < 2 * STEPS - TILES)

        @block.tensor
        def _(pe):
            pe.sem_inc(s_s3, CREDIT_S3)

            def may_turn(bt, r):
                if r == 0:
                    pe.wait_ge(s_rows, bt * 2 + 5)
                    pe.wait_ge(s_scal, bt * GROUPS + GROUPS)
                else:
                    pe.wait_ge(s_cols, (bt + 1) * 4 + r)

            def turn(r, bank):
                rows = x0_rows[:, :].rearrange("p (f d) -> p f d", d=D)
                for i in range(4):
                    mm = nc.tensor.transpose(ps[0:CYCLIC, bank, i * P:(i + 1) * P],
                                             rows[:, :, 4 * r + i], eye[:, :])
                mm.then_inc(s_turn, 1)

            def turn_scalars(gf, j):
                pe.wait_ge(s_const, 16 * 2)
                pe.wait_ge(s_scal, gf)
                if j == GROUPS:
                    pe.wait_ge(s_cols, gf + 4)
                for t in range(TILES):
                    at = (j % GROUPS * TILES + t) * P
                    mm = nc.tensor.transpose(ps[:, MISC_BANK, t * F:(t + 1) * F],
                                             x0_cols[0:F, at:at + P], eye[0:F, 0:F])
                mm.then_inc(s_st, 1)

            def cin1(gf, k, first=False):
                order = range(KT) if first else CIN1_ORDER
                if k == order[0] and not first:
                    pe.wait_ge(s_r1, gf)
                if k in SPLIT and not first:
                    i = SPLIT.index(k)
                    pe.wait_ge(*low_ready(gf, i))
                    passes = ((w0_high[:, i, :], prods_high[:, i, :]), (w0_low[:, i, :], prods_high[:, i, :]),
                              (w0_high[:, i, :], prods_low[:, i, :]))
                else:
                    pe.wait_ge(s_prod, gf * KT + k + 1)
                    passes = ((w0[:, k, :], prods[0:KR, k, :]),)
                for n, (w, x) in enumerate(passes):
                    mm = nc.tensor.matmul(ps[:, X1_BANK, :], w, x, start=(k == order[0] and n == 0),
                                          stop=(k == order[-1] and n == len(passes) - 1))
                if k == order[-1]:
                    mm.then_inc(s_x1, 1)

            def cin2(bt, u, q, turn_next):
                n = BANKS * u + q
                old = n - RING
                if old % BANKS in ACT_BANKS:
                    pe.wait_ge(s_ya, bt * (STEPS * NA) + banks_before(ACT_BANKS, old + 1) + CREDIT_A)
                else:
                    pe.wait_ge(s_mac, bt * (STEPS * MACS) + macs_before(old + 1) + CREDIT_MAC)
                if u % TILES == 0 and q == 0:
                    pe.wait_ge(s_x1h, bt * GROUPS + u // TILES + 1)
                    pe.wait_ge(s_x1l, bt * GROUPS + u // TILES + 1)
                par, at = u // TILES % 2, u % TILES * P
                width = min(FB, F - FB * q) * G
                y = ps[:, n % RING, 0:width]
                high = w1_high[:, q * FB * G:q * FB * G + width]
                low = w1_low[:, q * FB * G:q * FB * G + width]
                nc.tensor.matmul(y, x1_high[:, par, at:at + P], high, start=True, stop=False)
                nc.tensor.matmul(y, x1_high[:, par, at:at + P], low, start=False, stop=False)
                if turn_next:
                    may_turn(bt, TURNS.index((u, q)))
                nc.tensor.matmul(y, x1_low[:, par, at:at + P], high, start=False, stop=True) \
                    .then_inc(s_y, 1)

            def sum_s3(bt, u):
                pe.wait_ge(s_x2, bt * STEPS + u - 1 + CREDIT_X2)
                pe.wait_ge(s_diag, bt * STEPS + u - 1)
                pe.wait_ge(s_s3e, bt * STEPS + u - 2 + CREDIT_S3E)
                nc.tensor.matmul(ps[:, S3_BANK, 0:TB * FX], x2[:, u % 2, :],
                                 x0_diag[:, u % 2].rearrange("p b f -> p (b f)"),
                                 start=True, stop=True).then_inc(s_s3, 1)

            def cin3(bt, lo, hi, scalars=NGROUP):
                if lo == 0:
                    pe.wait_ge(s_s3e, bt * STEPS + STEPS + CREDIT_S3E)
                    pe.wait_ge(s_scal, scalars)
                for f in range(lo, hi):
                    mm = nc.tensor.matmul(ps[:, MISC_BANK, 0:BATCH], w2[:, f, :], s3[:, f, :],
                                          start=(f == 0), stop=(f == F - 1))
                if hi == F:
                    mm.then_inc(s_l3, 1)

            def prologue():
                pe.wait_ge(s_const, 16 * 2)
                pe.wait_ge(s_top, 16 * 7)
                for c in range(NBATCH // 4):
                    for i in range(4):
                        mm = nc.tensor.transpose(ps[0:DENSE, c, i * P:(i + 1) * P],
                                                 dense_rows[:, 4 * c + i, :], eye[:, :])
                    mm.then_inc(s_den, 1)
                pe.wait_ge(s_dene, NBATCH // 4)
                pe.wait_ge(s_rows, 3)
                for r in range(4):
                    turn(r, r)
                pe.wait_ge(s_cols, 1)
                turn_scalars(0, 0)
                pe.wait_ge(s_w0s, 1)
                for k in range(KT):
                    cin1(0, k, True)
                pe.wait_ge(s_w0h, NS)
                pe.wait_ge(s_w0l, NS)
                pe.wait_ge(s_w1h, W1_CHUNKS)
                pe.wait_ge(s_w1l, W1_CHUNKS)
                pe.wait_ge(s_cols, 4)
                pe.wait_ge(s_w2, 16)

            def step(bt, u, last):
                tile, j = u % TILES, u // TILES + 1
                front = not (last and j == GROUPS)
                gf = bt * GROUPS + j
                for q in range(BANKS):
                    turns = not last and (u, q) in TURNS
                    if (tile, q) == SCALARS and j == 2:
                        pe.wait_ge(s_r, bt * 2 + CREDIT_R)
                    cin2(bt, u, q, turns)
                    if q == S3_AT and u >= 2:
                        sum_s3(bt, u)
                    if turns:
                        turn(TURNS.index((u, q)), MISC_BANK)
                    if front and (tile, q) == SCALARS:
                        turn_scalars(gf, j)
                    if front and (tile, q) in CIN1:
                        n = CIN1.index((tile, q))
                        if n == KT - 1 and j == GROUPS - 1 and not last:
                            pe.wait_ge(s_cols, bt * 4 + 8)
                        cin1(gf, CIN1_ORDER[n])
                    if u == STEPS + 1 and q in CIN3:
                        part = CIN3.index(q)
                        cin3(bt, F * part // len(CIN3), F * (part + 1) // len(CIN3), gf + 1)

            def layer1(h):
                cols = slice(h * 512, (h + 1) * 512)
                terms1 = [(wt1_dense, dense_t)] + [(wt1[:, k, :], x) for k, x in enumerate((r1, r2, r3))]
                for c, bank in enumerate(L1_BANKS[h]):
                    if h == 0 and bank < RING:
                        pe.wait_ge(s_ya, NBATCH * STEPS * NA + CREDIT_A)
                        pe.wait_ge(s_mac, NBATCH * STEPS * MACS + CREDIT_MAC)
                    for k, (w, x) in enumerate(terms1):
                        mm = nc.tensor.matmul(ps[:, bank, :], w[:, c * P:(c + 1) * P], x[:, cols],
                                              start=(k == 0), stop=(k == len(terms1) - 1))
                    mm.then_inc(s_h1, 1)

            def layer2(h):
                for c, bank in enumerate(L2_BANKS[h]):
                    for k in range(H1 // P):
                        if c == 0:
                            pe.wait_ge(s_h1e, 4 * h + k + 1)
                        mm = nc.tensor.matmul(ps[:, bank, :], wt2[:, k, c * P:(c + 1) * P],
                                              h1[:, h, k, :], start=(k == 0), stop=(k == H1 // P - 1))
                    mm.then_inc(s_h2, 1)

            def layer3(h):
                for k in range(H2 // P):
                    pe.wait_ge(s_h2e, 2 * h + k + 1)
                    mm = nc.tensor.matmul(ps[0:1, L3_BANKS[h], :], wt3[:, k:k + 1], h2[:, h, k, :],
                                          start=(k == 0), stop=(k == H2 // P - 1))
                mm.then_inc(s_out, 1)

            def tail(bt):
                sum_s3(bt, STEPS)
                pe.wait_ge(s_r1, NGROUP)
                layer1(0)
                sum_s3(bt, STEPS + 1)
                layer2(0)
                cin3(bt, 0, F)
                layer3(0)
                pe.wait_ge(s_r, 2 * NBATCH + CREDIT_R)
                layer1(1)
                layer2(1)
                layer3(1)

            prologue_then_batches(pe, step, prologue, tail)

        @block.scalar
        def _(act):
            act.dma_start(eye[:, :], c_eye[:, :]).then_inc(s_const, 16)
            act.dma_start(mask[:, :], c_mask[:, :]).then_inc(s_const, 16)
            act.dma_start(wt1[:, :, :], w_top1[0:3 * P, :].rearrange("(k p) n -> p k n", p=P)) \
                .then_inc(s_top, 16)
            act.dma_start(wt1_dense[:, :], w_top1[3 * P:3 * P + DENSE, :]).then_inc(s_top, 16)
            act.dma_start(wt2[:, :, :], w_top2.rearrange("(k p) n -> p k n", p=P)).then_inc(s_top, 16)
            act.dma_start(wt3[:, :], w_top3[:, :]).then_inc(s_top, 16)
            act.dma_start(bt1[:, :], b_top1[:, :]).then_inc(s_top, 16)
            act.dma_start(bt2[:, :], b_top2[:, :]).then_inc(s_top, 16)
            act.dma_start(dense_rows[:, :, :], dense_ctx.rearrange("(c p) k -> p c k", p=P)) \
                .then_inc(s_top, 16)
            act.sem_inc(s_ya, CREDIT_A)
            act.sem_inc(s_s3e, CREDIT_S3E)
            act.sem_inc(s_r, CREDIT_R)

            def put_aside(bt):
                act.wait_ge(s_gather, (bt + 1) * (16 * F))
                rows = x0_in[:, :, :].rearrange("p f d -> p (f d)")
                nc.scalar.activation(x0_rows[:, 0:SPT * F * D].rearrange("p (t x) -> p t x", t=SPT),
                                     rows.unsqueeze(1).to_broadcast([P, SPT, F * D]), ACT.Copy).then_inc(s_rows, 1)
                nc.scalar.activation(x0_rows[:, SPT * F * D:], rows[:, 0:(CYCLIC - SPT * F) * D],
                                     ACT.Copy).then_inc(s_rows, 1)

            def store_cols(bt, r):
                if r == 0:
                    for moved in s_second:
                        act.wait_ge(moved, bt * (GROUPS * 16))
                act.wait_ge(s_turn, bt * 4 + r + 1)
                nc.scalar.activation(
                    x0_cols[:, :].rearrange("k (b d) -> k d b", d=D)[:, 4 * r:4 * r + 4, :],
                    ps[0:CYCLIC, MISC_BANK, :].rearrange("k (d b) -> k d b", d=4), ACT.Copy).then_inc(s_cols, 1)

            def store_first_cols(samples, n):
                act.wait_ge(s_turn, 4)
                nc.scalar.activation(
                    x0_cols[:, :].rearrange("k (b d) -> k d b", d=D)[:, :, samples],
                    ps[0:CYCLIC, 0:4, :].rearrange("k r (d b) -> k (r d) b", d=4)[:, :, samples],
                    ACT.Copy).then_inc(s_cols, n)

            def store_scalars(gf, j, guard):
                act.wait_ge(s_st, gf + 1)
                if guard:
                    act.wait_ge(s_diag, (gf - 1) * TILES)
                nc.scalar.activation(x0_scal[:, j % 2, :, 0:F],
                                     ps[:, MISC_BANK, 0:TILES * F].rearrange("p (t f) -> p t f", f=F),
                                     ACT.Copy).then_inc(s_scal, 1)

            def split_high(gf, i):
                act.wait_ge(s_prod, gf * KT + SPLIT[i] + 1)
                nc.scalar.activation(prods_high[:, i, :], prods[0:KR, SPLIT[i], :], ACT.Copy).then_inc(s_high, 1)

            def store_x1(gf, j):
                act.wait_ge(s_x1, gf + 1)
                nc.scalar.activation(x1_high[:, j % 2, :], ps[:, X1_BANK, :], ACT.Copy).then_inc(s_x1h, 1)

            def scale(bt, u, q):
                if q == ACT_BANKS[0]:
                    act.wait_ge(s_x2, bt * STEPS + u - 1 + CREDIT_X2)
                    if u % TILES == 0:
                        act.wait_ge(s_scal, bt * GROUPS + u // TILES + 1)
                act.wait_ge(s_y, bt * (STEPS * BANKS) + BANKS * u + q + 1)
                for i in range(FB):
                    f = FB * q + i
                    op = nc.scalar.activation(
                        terms[:, u % 2, FB * ACT_BANKS.index(q) + i, :],
                        ps[:, (BANKS * u + q) % RING, i * G:(i + 1) * G], ACT.Copy,
                        scale=x0_scal[:, u // TILES % 2, u % TILES, f:f + 1])
                op.then_inc(s_ya, 1)

            def store_s3(bt, u):
                if u == 2:
                    act.wait_ge(s_r, bt * 2 + CREDIT_R)
                act.wait_ge(s_s3, bt * STEPS + u - 1 + CREDIT_S3)
                at = (u - 2) * TB
                nc.scalar.activation(s3[:, :, at:at + TB],
                                     ps[:, S3_BANK, 0:TB * FX].rearrange("p (b f) -> p f b", f=FX),
                                     ACT.Copy).then_inc(s_s3e, 1)

            def store_r(bt):
                act.wait_ge(s_s3e, bt * STEPS + STEPS + CREDIT_S3E)
                nc.scalar.activation(r2[:, bass.ds(bt * BATCH, BATCH)], s3[:, F, :], ACT.Copy).then_inc(s_r, 1)
                act.wait_ge(s_l3, bt + 1)
                nc.scalar.activation(r3[:, bass.ds(bt * BATCH, BATCH)], ps[:, MISC_BANK, 0:BATCH],
                                     ACT.Copy).then_inc(s_r, 1)

            def prologue():
                act.wait_ge(s_w0s, 1)
                for i, k in enumerate(SPLIT):
                    nc.scalar.activation(w0_high[:, i, :], w0[:, k, :], ACT.Copy).then_inc(s_w0h, 1)
                n = F // W1_CHUNKS * G
                for c in range(W1_CHUNKS):
                    act.wait_ge(s_w1[c], 16)
                    nc.scalar.activation(w1_high[:, c * n:(c + 1) * n], w1_raw[:, c * n:(c + 1) * n],
                                         ACT.Copy).then_inc(s_w1h, 1)
                for c in range(NBATCH // 4):
                    act.wait_ge(s_den, c + 1)
                    nc.scalar.activation(dense_t[:, c * 512:(c + 1) * 512], ps[0:DENSE, c, :],
                                         ACT.Copy).then_inc(s_dene, 1)
                act.wait_ge(s_gather, 16 * F)
                nc.scalar.activation(
                    x0_rows[:, 0:(SPT - 1) * F * D].rearrange("p (t x) -> p t x", t=SPT - 1),
                    x0_in[:, :, :].rearrange("p f d -> p (f d)").unsqueeze(1).to_broadcast([P, SPT - 1, F * D]),
                    ACT.Copy).then_inc(s_rows, 1)
                store_first_cols(slice(0, GCOLS // D), 1)
                act.wait_ge(s_ones, 1)
                store_scalars(0, 0, False)
                store_first_cols(slice(GCOLS // D, BATCH), 3)
                store_x1(0, 0)

            def step(bt, u, last):
                tile, j = u % TILES, u // TILES + 1
                front = not (last and j == GROUPS)
                gf = bt * GROUPS + j
                for q in range(BANKS):
                    if q in ACT_BANKS:
                        scale(bt, u, q)
                    if q == S3_AT + 1 and u >= 2:
                        store_s3(bt, u)
                    if not last and (u, q) == ROWS_AT:
                        put_aside(bt + 1)
                    if not last and (u, q) in TURNS:
                        store_cols(bt + 1, TURNS.index((u, q)))
                    if front and (tile, q) == SCALARS:
                        store_scalars(gf, j, True)
                    if front and (tile, q) in HIGHS:
                        split_high(gf, HIGHS.index((tile, q)))
                    if front and (tile, q) == STORE_X1:
                        store_x1(gf, j)
                if u == STEPS + 1:
                    store_r(bt)

            def store_h1(h):
                for c, bank in enumerate(L1_BANKS[h]):
                    act.wait_ge(s_h1, 4 * h + c + 1)
                    nc.scalar.activation(h1[:, h, c, :], ps[:, bank, :], ACT.Relu,
                                         bias=bt1[:, c:c + 1]).then_inc(s_h1e, 1)

            def store_h2(h):
                for c, bank in enumerate(L2_BANKS[h]):
                    act.wait_ge(s_h2, 2 * h + c + 1)
                    nc.scalar.activation(h2[:, h, c, :], ps[:, bank, :], ACT.Relu,
                                         bias=bt2[:, c:c + 1]).then_inc(s_h2e, 1)

            def store_y(h):
                act.wait_ge(s_out, h + 1)
                nc.scalar.activation(y_row[:, h * 512:(h + 1) * 512], ps[0:1, L3_BANKS[h], :],
                                     ACT.Copy).then_inc(s_oute, 1)

            def tail(bt):
                store_s3(bt, STEPS)
                store_h1(0)
                store_s3(bt, STEPS + 1)
                store_h2(0)
                store_r(bt)
                store_y(0)
                store_h1(1)
                store_h2(1)
                store_y(1)

            prologue_then_batches(act, step, prologue, tail)

        @block.vector
        def _(dve):
            dve.sem_inc(s_mac, CREDIT_MAC)

            def multiply(bt, j, k):
                if k == 0:
                    dve.wait_ge(s_first[j % 2], (bt * (GROUPS // 2) + j // 2 + 1) * (16 * SPT))
                else:
                    dve.wait_ge(s_second[k - 1], (bt * GROUPS + j + 1) * 16)
                at = j % GROUPS * GCOLS
                second = prods[0:KR, k, :] if k else x0_cols[0:KR, at:at + GCOLS]
                nc.vector.tensor_tensor(prods[0:KR, k, :], second, x0_first[:, j % 2, :], ALU.mult) \
                    .then_inc(s_prod, 1)

            def split_x1(gf, j):
                dve.wait_ge(s_x1h, gf + 1)
                nc.vector.tensor_tensor(x1_low[:, j % 2, :], ps[:, X1_BANK, :],
                                        x1_high[:, j % 2, :].bitcast(F32), ALU.subtract).then_inc(s_x1l, 1)
                nc.vector.tensor_reduce(r1[:, bass.ds(gf * (GCOLS // D), GCOLS // D)],
                                        ps[:, X1_BANK, :].rearrange("p (b d) -> p b d", d=D),
                                        AX_X, ALU.add).then_inc(s_r1, 1)

            def mac(bt, u, q):
                if q == DVE_BANKS[0]:
                    dve.wait_ge(s_ya, bt * (STEPS * NA) + NA * u + 1 + CREDIT_A)
                    if u % TILES == 0:
                        dve.wait_ge(s_scal, bt * GROUPS + u // TILES + 1)
                dve.wait_ge(s_y, bt * (STEPS * BANKS) + BANKS * u + q + 1)
                done = macs_before(q)
                for i in range(min(FB, F - FB * q)):
                    f, n = FB * q + i, done + i
                    acc = terms[:, u % 2, n % CHAINS, :]
                    y = ps[:, (BANKS * u + q) % RING, i * G:(i + 1) * G]
                    x0 = x0_scal[:, u // TILES % 2, u % TILES, f:f + 1]
                    if n >= CHAINS:
                        dve.wait_ge(s_mac, bt * (STEPS * MACS) + MACS * u + n - CHAINS + 1 + CREDIT_MAC)
                    nc.vector.scalar_tensor_tensor(out=acc, in0=y, scalar=x0, in1=acc, op0=ALU.mult,
                                                   op1=ALU.add).then_inc(s_mac, 1)

            def diagonal(bt, u):
                dve.wait_ge(s_s3, bt * STEPS + u - 2 + CREDIT_S3)
                t = u - 1
                nc.vector.tensor_tensor(
                    x0_diag[:, t % 2],
                    x0_scal[:, t // TILES % 2, t % TILES, :].unsqueeze(1).to_broadcast([P, TB, FX]),
                    mask[:, :].unsqueeze(2).to_broadcast([P, TB, FX]), ALU.mult).then_inc(s_diag, 1)

            def prologue():
                nc.vector.memset(x0_scal[:, :, :, :], 1.0).then_inc(s_ones, 1)
                dve.wait_ge(s_w0, 32)
                nc.vector.tensor_tensor(w0[:, :, :].rearrange("r k m -> r (k m)"), w0_a, w0_b, ALU.add) \
                    .then_inc(s_w0s, 1)
                dve.wait_ge(s_w0h, NS)
                for i, k in enumerate(SPLIT):
                    nc.vector.tensor_tensor(w0_low[:, i, :], w0[:, k, :], w0_high[:, i, :].bitcast(F32),
                                            ALU.subtract).then_inc(s_w0l, 1)
                n = F // W1_CHUNKS * G
                for c in range(W1_CHUNKS):
                    dve.wait_ge(s_w1h, c + 1)
                    nc.vector.tensor_tensor(w1_low[:, c * n:(c + 1) * n], w1_raw[:, c * n:(c + 1) * n],
                                            w1_high[:, c * n:(c + 1) * n].bitcast(F32), ALU.subtract) \
                        .then_inc(s_w1l, 1)
                dve.wait_ge(s_gather, 16 * F)
                rows = x0_in[:, :, :].rearrange("p f d -> p (f d)")
                for c in (SPT - 1, SPT):
                    at, n = c * F * D, min(F, CYCLIC - c * F) * D
                    nc.vector.tensor_copy(x0_rows[:, at:at + n], rows[:, 0:n]).then_inc(s_rows, 1)
                for k in range(KT):
                    multiply(0, 0, k)
                split_x1(0, 0)

            def step(bt, u, last):
                tile, j = u % TILES, u // TILES + 1
                front = not (last and j == GROUPS)
                gf = bt * GROUPS + j
                for q in range(BANKS):
                    if q in DVE_BANKS:
                        mac(bt, u, q)
                    if q == 2 and u >= 1:
                        diagonal(bt, u)
                    if front and (tile, q) in PRODUCTS:
                        multiply(bt, j, PRODUCTS.index((tile, q)))
                    for i, at in DVE_LOWS.items():
                        if front and (tile, q) == at:
                            split_low(dve, gf, i)
                    if front and (tile, q) == SPLIT_X1:
                        split_x1(gf, j)

            prologue_then_batches(dve, step, prologue, lambda bt: diagonal(bt, STEPS))


TOP = ("W_top1", "b_top1", "W_top2", "b_top2", "W_top3")


def kernel(**inputs):
    import concourse.bacc as bacc
    from concourse.bass_utils import run_bass_kernel_spmd

    rows, mirror, apart = pair_rows()
    f0 = np.asarray(inputs["L0_rec_f0"])
    w0_pair = np.zeros((KT, SPT, F, G), f0.dtype)
    w0_mirror = np.zeros((KT, SPT, F, G), f0.dtype)
    there, mirrored = apart < SHIFTS, (apart < SHIFTS) & (apart > 0)
    w0_pair[there] = f0[rows[there]]
    w0_mirror[mirrored] = f0[mirror[mirrored]]
    c_mask, c_eye = layout_constants()
    named = {"dense_ctx": inputs["dense_ctx"], "ids": inputs["ids"]}
    named |= {f"tbl_{f}": inputs[f"tbl_{f}"] for f in range(F)}
    named |= {name: inputs[name] for name in TOP}
    for name in ("b_top1", "b_top2", "W_top3"):
        named[name] = np.asarray(inputs[name]).reshape(-1, P).T
    named |= {"w0_pair": w0_pair.reshape(KT, KR, G), "w0_mirror": w0_mirror.reshape(KT, KR, G),
              "f1": inputs["L0_rec_f1"], "f2": inputs["L0_rec_f2"],
              "c_mask": c_mask, "c_eye": c_eye}
    nc = bacc.Bacc("TRN2", target_bir_lowering=False, num_devices=1)
    arrays, ap = {}, {}
    for name, x in named.items():
        a = np.ascontiguousarray(x)
        arrays["in_" + name] = a
        ap[name] = nc.dram_tensor("in_" + name, a.shape, mybir.dt.from_np(a.dtype), kind="ExternalInput").ap()
    out = nc.dram_tensor("out_y", (B, 1), F32, kind="ExternalOutput").ap()
    cin_tower(nc, ap["dense_ctx"], ap["ids"], [ap[f"tbl_{f}"] for f in range(F)],
              *[ap[name] for name in TOP], ap["w0_pair"], ap["w0_mirror"], ap["f1"], ap["f2"],
              ap["c_mask"], ap["c_eye"], out)
    r = run_bass_kernel_spmd(nc, [arrays], core_ids=[0])
    return r.results[0]["out_y"]
```
